# Optimizing a Trainium2 kernel written in Bass

```python
import numpy as np
import jax
import jax.numpy as jnp

def _softmax(x, axis=-1):
    return jax.nn.softmax(x, axis=axis)

def _gelu(x):
    return jax.nn.gelu(x, approximate=True)

def _silu(x):
    return jax.nn.silu(x)

def _sigmoid(x):
    return jax.nn.sigmoid(x)

def _layernorm(x, axis=-1, eps=1e-05):
    m = jnp.mean(x, axis=axis, keepdims=True)
    v = jnp.var(x, axis=axis, keepdims=True)
    return (x - m) / jnp.sqrt(v + eps)

def _scatter_add(tgt, idx, src, axis=0):
    return tgt.at[idx].add(src)

def _segment_sum(src, seg, n):
    return jax.ops.segment_sum(src, seg, n)
kernel_name = 'mk_flamingo_gated_d1_seqx_r8_d2055e'

def setup_inputs(seed: int=0):
    np.random.seed(seed)
    _w = jnp.asarray

    def _rec_inputs():
        import jax
        import jax.numpy as jnp
        _rk = jax.random.key(seed)
        x = -0.0002928 + 1 * jax.random.normal(jax.random.fold_in(_rk, 1), (4, 256, 128), jnp.float32)
        _lenS = 256 - jax.random.randint(jax.random.fold_in(_rk, 7), (4,), 0, max(1, 256 // 4) + 1, jnp.int32)
        _lenS2 = 1601 - jax.random.randint(jax.random.fold_in(_rk, 8), (4,), 0, max(1, 1601 // 4) + 1, jnp.int32)
        _ctx_1024P = jax.random.normal(jax.random.fold_in(_rk, 11), (4, 16, 128), jnp.float32)
        _ctx_1024c = jax.random.dirichlet(jax.random.fold_in(_rk, 511), 0.3 * jnp.ones((16,), jnp.float32), (4, 1601))
        _ctx_1024t = jnp.einsum('bsk,bkd->bsd', _ctx_1024c, _ctx_1024P)
        _ctx_1024t = _ctx_1024t * jax.lax.rsqrt(jnp.mean(jnp.square(_ctx_1024t)) + 1e-12) * 0.953939
        ctx_1024 = -1.39393e-06 + 0.999914 * (_ctx_1024t + 0.3 * jax.random.normal(jax.random.fold_in(_rk, 611), (4, 1601, 128), jnp.float32))
        _validS = jnp.arange(256)[None, :] < _lenS[:, None]
        _validS2 = jnp.arange(1601)[None, :] < _lenS2[:, None]
        _causal = jnp.tril(jnp.ones((256, 256), dtype=bool))
        mask_1x1xSxS2_if1 = jnp.where(jnp.ones((1, 1, 256, 1601), dtype=bool), 1, 0).astype(jnp.int32)
        _g = jax.random.normal(jax.random.fold_in(_rk, 9001), (2, 1), jnp.float32)
        _g = jnp.sign(_g) * jnp.maximum(jnp.abs(_g), 1.0) + (_g == 0) * 1.0
        g_xattn = _g[0]
        g_ffn = _g[1]
        return (x, ctx_1024, mask_1x1xSxS2_if1, g_xattn, g_ffn)
    x, ctx_1024, mask_1x1xSxS2_if1, g_xattn, g_ffn = _rec_inputs()

    def _L0_xattn_setup():
        import jax, jax.numpy as jnp
        import numpy as np
        import math
        H = 16
        D_MODEL = 128
        B, S = (2, 256)
        key = jax.random.key(seed)
        ks = jax.random.split(key, 7)
        q = jax.random.normal(ks[0], (B, S, D_MODEL), dtype=jnp.float32)
        k = jax.random.normal(ks[1], (B, S, D_MODEL), dtype=jnp.float32)
        v = jax.random.normal(ks[2], (B, S, D_MODEL), dtype=jnp.float32)
        mask = jnp.ones((1, 1, S, S), dtype=jnp.int32)
        sc = 1.0 / math.sqrt(D_MODEL)
        W_Q = jax.random.normal(ks[3], (D_MODEL, D_MODEL), dtype=jnp.float32) * sc
        W_K = jax.random.normal(ks[4], (D_MODEL, D_MODEL), dtype=jnp.float32) * sc
        W_V = jax.random.normal(ks[5], (D_MODEL, D_MODEL), dtype=jnp.float32) * sc
        W_T = jax.random.normal(ks[6], (D_MODEL, D_MODEL), dtype=jnp.float32) * sc
        return {'q': q, 'k': k, 'v': v, 'mask': mask, 'W_Q': W_Q, 'W_K': W_K, 'W_V': W_V, 'W_T': W_T}
    _L0_xattn_all = _L0_xattn_setup()
    _L0_xattn_in = {k: v for k, v in _L0_xattn_all.items() if k in ('W_Q', 'W_K', 'W_V', 'W_T')}
    del _L0_xattn_all

    def _L0_ffn_setup():
        import jax, jax.numpy as jnp
        import numpy as np
        HIDDEN = 128
        INTER = 256
        NUM_EXPERTS = 8
        TOPK = 2
        STD = 0.02
        key = jax.random.key(seed)
        k1, k2, k3, k4 = jax.random.split(key, 4)
        return {'hidden_states': jax.random.normal(k1, (1, 256, HIDDEN), dtype=jnp.float32), 'w1': jax.random.normal(k2, (NUM_EXPERTS, 2 * INTER, HIDDEN), dtype=jnp.float32) * STD, 'w2': jax.random.normal(k3, (NUM_EXPERTS, HIDDEN, INTER), dtype=jnp.float32) * STD, 'router_w': jax.random.normal(k4, (NUM_EXPERTS, HIDDEN), dtype=jnp.float32) * STD}
    _L0_ffn_all = _L0_ffn_setup()
    _L0_ffn_in = {k: v for k, v in _L0_ffn_all.items() if k in ('w1', 'w2', 'router_w')}
    del _L0_ffn_all
    return {'x': x, 'ctx_1024': ctx_1024, 'mask_1x1xSxS2_if1': mask_1x1xSxS2_if1, 'g_xattn': g_xattn, 'g_ffn': g_ffn, 'L0_xattn_W_Q': _L0_xattn_in['W_Q'], 'L0_xattn_W_K': _L0_xattn_in['W_K'], 'L0_xattn_W_V': _L0_xattn_in['W_V'], 'L0_xattn_W_T': _L0_xattn_in['W_T'], 'L0_ffn_w1': _L0_ffn_in['w1'], 'L0_ffn_w2': _L0_ffn_in['w2'], 'L0_ffn_router_w': _L0_ffn_in['router_w']}

def reference(x, ctx_1024, mask_1x1xSxS2_if1, g_xattn, g_ffn, L0_xattn_W_Q, L0_xattn_W_K, L0_xattn_W_V, L0_xattn_W_T, L0_ffn_w1, L0_ffn_w2, L0_ffn_router_w):
    import jax
    import jax.numpy as jnp

    def _L0_xattn_ref(q, k, v, mask, W_Q, W_K, W_V, W_T):
        import jax, jax.numpy as jnp
        import numpy as np
        import math
        H = 16
        D_MODEL = 128
        B, S = (2, 256)

        def split_heads(x):
            Bq, Sq, Dq = x.shape
            return x.reshape(Bq, Sq, H, Dq // H).transpose(0, 2, 1, 3)
        Q = split_heads(q @ W_Q)
        K = split_heads(k @ W_K)
        V = split_heads(v @ W_V)
        d_k = Q.shape[-1]
        score = jnp.einsum('bhqd,bhkd->bhqk', Q, K) / math.sqrt(d_k)
        score = jnp.where(mask == 0, jnp.float32(-1000000000.0), score)
        attn = jax.nn.softmax(score, axis=-1)
        out = jnp.einsum('bhqk,bhkd->bhqd', attn, V)
        out = out.transpose(0, 2, 1, 3).reshape(q.shape[0], q.shape[1], D_MODEL)
        return out @ W_T

    def _L0_ffn_ref(hidden_states, w1, w2, router_w):
        import jax, jax.numpy as jnp
        import numpy as np
        HIDDEN = 128
        INTER = 256
        NUM_EXPERTS = 8
        TOPK = 2
        STD = 0.02
        orig_shape = hidden_states.shape
        dtype = hidden_states.dtype
        x = hidden_states.reshape(-1, orig_shape[-1])
        E = w1.shape[0]
        gating = x @ router_w.T
        probs = jax.nn.softmax(gating.astype(jnp.float32), axis=-1)
        topk_w, sel = jax.lax.top_k(probs, TOPK)
        topk_w = topk_w.astype(dtype)
        combine = (jax.nn.one_hot(sel, E, dtype=dtype) * topk_w[..., None]).sum(axis=1)
        h = jnp.einsum('td,eid->tei', x, w1)
        gate = jax.nn.silu(h[..., :INTER])
        y = h[..., INTER:] * gate
        out = jnp.einsum('tei,ehi,te->th', y, w2, combine)
        return out.reshape(orig_shape)
    x = x + jnp.tanh(g_xattn[0]) * _L0_xattn_ref(_layernorm(x, axis=-1), ctx_1024, ctx_1024, mask_1x1xSxS2_if1, L0_xattn_W_Q, L0_xattn_W_K, L0_xattn_W_V, L0_xattn_W_T)
    x = x + jnp.tanh(g_ffn[0]) * _L0_ffn_ref(_layernorm(x, axis=-1), L0_ffn_w1, L0_ffn_w2, L0_ffn_router_w)
    return x

_drawn_inputs = setup_inputs


def setup_inputs(seed=0):
    import zlib

    import numpy as np

    out = dict(_drawn_inputs(seed))
    spreads = {}
    factors = {'L0_ffn_w1': 8.0, 'L0_ffn_w2': 8.0, 'L0_ffn_router_w': 8.0}
    for name, (base, spread) in spreads.items():
        noise = np.random.default_rng([zlib.crc32(name.encode()), seed]).standard_normal(out[name].shape)
        drawn = base * np.exp(spread * noise) if base else spread * noise
        out[name] = jnp.asarray(drawn.astype(out[name].dtype))
    for name, factor in factors.items():
        out[name] = (out[name] * factor).astype(out[name].dtype)
    return out
```

```python
from contextlib import ExitStack

import numpy as np

import concourse.bass as bass
from concourse import mybir

FP32, BF16 = mybir.dt.float32, mybir.dt.bfloat16
I32, U32 = mybir.dt.int32, mybir.dt.uint32
ALU, ACT, AX = mybir.AluOpType, mybir.ActivationFunctionType, mybir.AxisListType

P = 128
B, S, D = 4, 256, 128
SK = 1601
H, DH = 16, 8
E, INTER = 8, 256
QH = 4
NQ = H // QH
QT = S // P
KT = -(-SK // P)
TAIL = SK - (KT - 1) * P
PARTS = 3
ROWS = PARTS * PARTS * DH
NEG = ROWS
KR = ROWS + PARTS
BANK = 512
CH = -(-SK // BANK)
CW = [min(BANK, SK - c * BANK) for c in range(CH)]
CHUNKS = QH * QT * CH
STEPS = (KT + 1) // 2
SLOTS = QH * (STEPS - 1) + QH // 2
LEAD = 8
TILES = INTER // P
NT = E * TILES
VW = 32
EPS = 1e-5
MASKED = -float(2 ** 100)
SCALE = 1.0 / float(np.sqrt(DH))

S_PVTAIL, S_OCOPY, S_OTR, S_ONORM = 1, 3, 6, 8
S_MTR, S_MCOPY = 21, 22
S_HT, S_HTCOPY, S_PROJ, S_X1, S_XN, S_XNTR, S_XNCOPY, S_ROUTE, S_TOP = 9, 11, 13, 14, 16, 18, 20, 22, 24
TILE_STRIDE = 4
TPU = 6


def hold(eng, sem, n):
    if not isinstance(n, int) or n > 0:
        eng.wait_ge(sem, n)


class Chain:

    def __init__(self, eng, sem, start=0):
        self.eng, self.sem, self.n = eng, sem, start

    def link(self, ins):
        ins.then_inc(self.sem, 1)
        self.n = self.n + 1
        self.eng.wait_ge(self.sem, self.n)


def following(b, q, by=1):
    return (b + (q + by) // NQ, (q + by) % NQ)


def max_chunks(slot):
    lo, hi = (CHUNKS * (slot + LEAD) // SLOTS, CHUNKS * (slot + 1 + LEAD) // SLOTS)
    return range(lo, hi)


FIRST_CHUNKS = CHUNKS * LEAD // SLOTS


def expert_tiles(q):
    return [(n, TILE_STRIDE * (n % TPU) + 1) for n in range(NT) if 1 + n // TPU == q]


def block_kernel(nc, x, ctxT, mask, maskT, g_x, g_f, W_Q, W_K, W_V, W_T, w1T, w2T, rT, out):
    es = ExitStack()
    sb = lambda name, shape, dt: es.enter_context(nc.sbuf_tensor(name, shape, dt))
    ps = lambda name, dt=FP32: es.enter_context(nc.psum_tensor(name, [P, BANK * 4 // (2 if dt == BF16 else 4)], dt))
    sem = lambda name: es.enter_context(nc.semaphore(name))

    with es:
        k_parts_dram = nc.dram_tensor("k_parts", [B, H, PARTS, DH, SK], BF16).ap()
        q_parts_dram = nc.dram_tensor("q_parts", [H, PARTS, PARTS, DH, B * S], BF16).ap()

        wq, wk, wv, wt = (sb(n, [P, D], FP32) for n in ("wq", "wk", "wv", "wt"))
        w1 = sb("w1", [P, E, 2 * INTER], FP32)
        w2 = sb("w2", [P, E, TILES, D], FP32)
        wr = sb("wr", [P, E], FP32)
        gates = sb("gates", [P, 2], FP32)
        gate_t = sb("gate_t", [P, 2], FP32)
        ctx_in = sb("ctx_in", [P, 2, SK], FP32)
        masked_q = sb("masked_q", [P, QT, SK], BF16)
        masked_k = sb("masked_k", [P, KT, S], BF16)
        row_masked = sb("row_masked", [P, 1], FP32)
        any_masked = sb("any_masked", [1, 1], I32)
        ident = sb("ident", [P, P], FP32)
        ident_b = sb("ident_b", [P, P], BF16)
        ident_neg = sb("ident_neg", [P, P], BF16)
        ones_col = sb("ones_col", [P, 1], FP32)
        iota_i = sb("iota_i", [P, E], I32)
        iota_f = sb("iota_f", [P, E], FP32)
        minus_half = sb("minus_half", [P, B * QT], FP32)
        xs = sb("xs", [P, B * QT, D], FP32)
        stats = sb("stats", [P, B * QT, 6], FP32)
        meanvar = sb("meanvar", [P, B * QT, 2], FP32)
        rstd = sb("rstd", [P, B * QT], FP32)
        split = sb("split", [P, PARTS, SK], BF16)
        rest = sb("rest", [P, 2, BANK], FP32)
        keys = [sb(f"keys{i}", [P, QH, SK], BF16) for i in range(NQ)]
        queries = [sb(f"queries{i}", [P, QH, S], BF16) for i in range(NQ)]
        values = sb("values", [P, B, KT, D], FP32)
        value_t = [sb(f"value_t{i}", [P, KT, QH, VW], FP32) for i in range(2)]
        probs = sb("probs", [P, 2 * QH, 2 * S], FP32)
        probs_tail = sb("probs_tail", [P, QH // 2, 2 * S], FP32)
        chunk_max = sb("chunk_max", [P, 2, QT, QH, CH], FP32)
        row_max = sb("row_max", [P, QT, QH], FP32)
        neg_max = sb("neg_max", [P, QT, QH], FP32)
        neg_rest = sb("neg_rest", [P, QT, QH], FP32)
        neg_parts = sb("neg_parts", [P, QT, PARTS, QH], BF16)
        neg_rows = sb("neg_rows", [PARTS * QH, S], BF16)
        head_outT = sb("head_outT", [P, S], FP32)
        denom = sb("denom", [P, QT, QH], FP32)
        heads = sb("heads", [P, QT, D], FP32)
        headsT = sb("headsT", [P, S], FP32)
        x_b = sb("x_b", [P, QT, D], FP32)
        x1 = sb("x1", [P, QT, D], FP32)
        xn2 = sb("xn2", [P, QT, D], FP32)
        xn2T = sb("xn2T", [P, S], FP32)
        stats2 = sb("stats2", [P, QT, 6], FP32)
        meanvar2 = sb("meanvar2", [P, QT, 2], FP32)
        rstd2 = sb("rstd2", [P, QT], FP32)
        logits = sb("logits", [P, QT, E], FP32)
        top = sb("top", [P, QT, 8], FP32)
        top_i = sb("top_i", [P, QT, 8], U32)
        top_f = sb("top_f", [P, QT, 8], FP32)
        rel = sb("rel", [P, QT, E], FP32)
        expo = sb("expo", [P, QT, E], FP32)
        first_hot = sb("first_hot", [P, QT, E], FP32)
        second_hot = sb("second_hot", [P, QT, E], FP32)
        total = sb("total", [P, QT], FP32)
        combine = sb("combine", [P, QT, E], FP32)
        th = sb("th", [P, 2, S], FP32)
        gated = sb("gated", [P, S], FP32)
        inner = sb("inner", [P, 4, S], FP32)
        mask_in = probs[:, :, :].rearrange("p a b -> p (a b)").bitcast(I32).rearrange(
            "p (g k) -> p g k", g=2)
        xn = inner[:, :, :].rearrange("p a b -> p (a b)").rearrange("p (t d) -> p t d", d=D)
        xnT = probs_tail[:, :, :].rearrange("p a b -> p (a b)")

        max_bank = [ps("max_bank0"), ps("max_bank1")]
        score_bank = [ps("score_bank0"), ps("score_bank1")]
        pv_bank = ps("pv_bank")
        up_bank = ps("up_bank")
        down_bank = ps("down_bank")
        misc_bank = ps("misc_bank")
        misc_b = misc_bank[:, :].bitcast(BF16)

        ld_x, ld_w, ld_fw, ld_mask = sem("ld_x"), sem("ld_w"), sem("ld_fw"), sem("ld_mask")
        ld_ctx = [sem("ld_ctx0"), sem("ld_ctx1")]
        const_ready, ident_ready, neg_ready = sem("const_ready"), sem("ident_ready"), sem("neg_ready")
        zeroed = sem("zeroed")
        rows_ready = sem("rows_ready")
        ln_step, rstd_ready, xn_ready = sem("ln_step"), sem("rstd_ready"), sem("xn_ready")
        xnT_ready, xnT_copied = sem("xnT_ready"), sem("xnT_copied")
        proj_ready, hi_ready, rest_ready, mid_ready, lo_ready = (
            sem("proj_ready"), sem("hi_ready"), sem("rest_ready"), sem("mid_ready"), sem("lo_ready"))
        v_ready, v_by_act, v_by_dve = sem("v_ready"), sem("v_by_act"), sem("v_by_dve")
        q_stored, k_stored, ones_rows = sem("q_stored"), sem("k_stored"), sem("ones_rows")
        mask_used, mask_done, flag_sum, flag_ready = (
            sem("mask_used"), sem("mask_done"), sem("flag_sum"), sem("flag_ready"))
        gate_step, gates_ready = sem("gate_step"), sem("gates_ready")
        ld_unit = [sem(f"ld_unit{i}") for i in range(NQ)]
        chunk_ready, chunk_used = sem("chunk_ready"), sem("chunk_used")
        max_ready, neg_step, neg_parts_ready = sem("max_ready"), sem("neg_step"), sem("neg_parts_ready")
        neg_T, neg_rows_ready, neg_in = sem("neg_T"), sem("neg_rows_ready"), sem("neg_in")
        scores_ready, probs_ready, pv_done = sem("scores_ready"), sem("probs_ready"), sem("pv_done")
        values_ready = sem("values_ready")
        out_copied, out_T, out_step, heads_ready = sem("out_copied"), sem("out_T"), sem("out_step"), sem("heads_ready")
        hT_ready, hT_copied, attn_ready = sem("hT_ready"), sem("hT_copied"), sem("attn_ready")
        x_b_in, tail_step, var_ready, rstd2_ready, xn2_ready = (
            sem("x_b_in"), sem("tail_step"), sem("var_ready"), sem("rstd2_ready"), sem("xn2_ready"))
        rstd2_step = sem("rstd2_step")
        xn2T_ready, xn2T_copied, route_ready = sem("xn2T_ready"), sem("xn2T_copied"), sem("route_ready")
        rel_ready, expo_ready, route_step = sem("rel_ready"), sem("expo_ready"), sem("route_step")
        up_ready, th_ready, gated_step, inner_ready = sem("up_ready"), sem("th_ready"), sem("gated_step"), sem("inner_ready")
        down_ready, down_used, out_stored = sem("down_ready"), sem("down_used"), sem("out_stored")

        block = es.enter_context(nc.Block())

        @block.sync
        def _(sp):
            x_rows = x.rearrange("b (t p) d -> p (b t) d", p=P)
            out_rows = out.rearrange("b (t p) d -> b p t d", p=P)

            def load_ctx(b):
                if b >= 2:
                    sp.wait_ge(proj_ready, 2 + CH * (b - 1))
                    sp.wait_ge(v_ready, 4 * (b - 1))
                sp.dma_start(ctx_in[:, b % 2, :], ctxT[b]).then_inc(ld_ctx[b % 2], 16)

            def load_unit(b, q):
                h0 = QH * q
                for c in range(PARTS):
                    rows = slice(c * PARTS * DH, (c + 1) * PARTS * DH)
                    sp.dma_start(keys[q][rows, :, :],
                                 k_parts_dram[b, h0:h0 + QH].rearrange("j p d k -> (p d) j k")).then_inc(ld_unit[q], 16)
                sp.dma_start(queries[q][0:ROWS, :, :],
                             q_parts_dram[h0:h0 + QH, :, :, :, bass.ds(b * S, S)].rearrange("j c p d t -> (c p d) j t")
                             ).then_inc(ld_unit[q], 16)

            def load_neg(b, q):
                sp.wait_ge(neg_rows_ready, NQ * b + q + 1)
                for p in range(PARTS):
                    sp.dma_start(queries[q][NEG + p:NEG + p + 1, :, :], neg_rows[p * QH:(p + 1) * QH, :]).then_inc(neg_in, 16)

            sp.dma_start(xs[:, :, :], x_rows).then_inc(ld_x, 16)
            sp.dma_start(wq[:, :], W_Q).then_inc(ld_w, 16)
            sp.dma_start(wk[:, :], W_K).then_inc(ld_w, 16)
            load_ctx(0)
            sp.dma_start(wv[:, :], W_V).then_inc(ld_w, 16)
            load_ctx(1)
            sp.wait_ge(rows_ready, 1)
            for i in range(NQ):
                sp.dma_start(keys[i][NEG:KR, :, :], keys[NQ - 1][0:PARTS, :, :]).then_inc(ones_rows, 16)
            sp.dma_start(gates[:, 0:1], g_x.rearrange("(o g) -> o g", o=1).broadcast_to([P, 1])).then_inc(ld_w, 16)
            sp.dma_start(gates[:, 1:2], g_f.rearrange("(o g) -> o g", o=1).broadcast_to([P, 1])).then_inc(ld_w, 16)
            sp.wait_ge(lo_ready, 2)
            for c in range(PARTS):
                for p in range(PARTS):
                    sp.dma_start(q_parts_dram[:, c, p], split[:, c, 0:B * S]).then_inc(q_stored, 16)
            for b in range(B):
                sp.wait_ge(lo_ready, 2 + CH * (b + 1))
                for p in range(PARTS):
                    sp.dma_start(k_parts_dram[b, :, p], split[:, p, :]).then_inc(k_stored, 16)
                if b + 2 < B:
                    load_ctx(b + 2)
                if b == 0:
                    sp.wait_ge(ones_rows, 16 * NQ)
                    sp.wait_ge(q_stored, 16 * PARTS * PARTS)
                    sp.wait_ge(k_stored, 16 * PARTS)
                    load_unit(0, 0)
                    load_unit(0, 1)
                    sp.dma_start(wt[:, :], W_T).then_inc(ld_fw, 16)
                    sp.dma_start(w1[:, :, :], w1T.rearrange("d (e i) -> d e i", e=E)).then_inc(ld_fw, 16)
                    sp.dma_start(w2[:, :, :, :], w2T.rearrange("e (t p) h -> p e t h", p=P)).then_inc(ld_fw, 16)
                    sp.dma_start(wr[:, :], rT).then_inc(ld_fw, 16)
            sp.wait_ge(k_stored, 16 * PARTS * B)
            load_neg(0, 0)

            def units(b, tail, attn, last):
                for q in range(NQ):
                    u = NQ * b + q
                    if q == 0 and tail:
                        if not isinstance(b, int) or b >= 2:
                            sp.wait_ge(down_used, E * (b - 1))
                            sp.dma_start(out_rows[b - 2], x1[:, :, :]).then_inc(out_stored, 16)
                        hold(sp, var_ready, b - 1)
                        sp.dma_start(x_b[:, :, :], x[b - 1].rearrange("(t p) d -> p t d", p=P)).then_inc(x_b_in, 16)
                    if not attn:
                        continue
                    if not (last and q >= NQ - 2):
                        hold(sp, scores_ready, SLOTS * (u - 1))
                        load_unit(*following(b, q, 2))
                    if not (last and q == NQ - 1):
                        load_neg(*following(b, q))

            units(0, False, True, False)
            units(1, True, True, False)
            with sp.Fori(2, B - 1) as b:
                units(b, True, True, False)
            units(B - 1, True, True, True)
            units(B, True, False, True)
            sp.wait_ge(down_used, E * B)
            sp.dma_start(out_rows[B - 1], x1[:, :, :]).then_inc(out_stored, 16)
            sp.wait_ge(out_stored, 16 * B)

        @block.gpsimd
        def _(pool):
            mask_v = mask.rearrange("(t p) k -> p t k", p=P)
            for t in range(QT):
                pool.dma_start(mask_in[:, t, 0:SK], mask_v[:, t, :]).then_inc(ld_mask, 16)
            nc.gpsimd.memset(ident[:, :], 0.0).then_inc(zeroed, 1)
            nc.gpsimd.memset(ident_b[:, :], 0.0).then_inc(zeroed, 1)
            nc.gpsimd.memset(ident_neg[:, :], 0.0).then_inc(zeroed, 1)
            pool.wait_ge(zeroed, 3)
            for m, fill in ((ident, 1.0), (ident_b, 1.0), (ident_neg, MASKED)):
                nc.gpsimd.affine_select(out=m[:, :], in_=m[:, :], compare_op=ALU.not_equal, fill=fill, base=0,
                                        pattern=[[-1, P]], channel_multiplier=1).then_inc(ident_ready, 1)
            nc.gpsimd.memset(ones_col[:, :], 1.0).then_inc(const_ready, 1)
            nc.gpsimd.memset(minus_half[:, :], -0.5).then_inc(const_ready, 1)
            nc.gpsimd.iota(iota_i[:, :], pattern=[[1, E]], base=0, channel_multiplier=0).then_inc(const_ready, 1)
            for i in range(2):
                nc.gpsimd.memset(value_t[i][:, :, :, :], 0.0).then_inc(const_ready, 1)
            pool.wait_ge(const_ready, 5)
            for i in range(2):
                nc.gpsimd.memset(value_t[i][:, :, :, DH:DH + 1], 1.0).then_inc(const_ready, 1)
            pool.wait_ge(ln_step, 2 * B * QT)
            chain = Chain(pool, rstd_ready)
            chain.link(nc.gpsimd.tensor_scalar(rstd[:, :], meanvar[:, :, 1], EPS, None, ALU.add))
            nc.gpsimd.tensor_tensor(rstd[:, :], rstd[:, :], minus_half[:, :], ALU.pow).then_inc(rstd_ready, 1)
            for i in range(2 + CH * B):
                c = (i - 2) % CH
                cols = slice(i * BANK, (i + 1) * BANK) if i < 2 else slice(c * BANK, c * BANK + CW[c])
                w = cols.stop - cols.start
                pool.wait_ge(mid_ready, i + 1)
                nc.gpsimd.tensor_tensor(split[:, 2, cols], rest[:, i % 2, 0:w], split[:, 1, cols],
                                        ALU.subtract).then_inc(lo_ready, 1)
                if i == 0:
                    for g in range(2):
                        pool.wait_ge(mask_used, g + 1)
                        n = 7 if g == 0 else KT - 1 - 7
                        pool.dma_start(mask_in[:, g, 0:n * S].rearrange("p (t q) -> p t q", q=S),
                                       maskT[g * 7 * P:(g * 7 + n) * P, :].rearrange("(t p) q -> p t q", p=P)
                                       ).then_inc(ld_mask, 16)
                    pool.dma_start(mask_in[0:TAIL, 1, (KT - 8) * S:(KT - 7) * S], maskT[(KT - 1) * P:SK, :]).then_inc(ld_mask, 16)

            def load_values(b, q):
                i, cols = q % 2, slice(q * QH * DH, (q + 1) * QH * DH)
                nc.gpsimd.tensor_copy(value_t[i][:, 0:KT - 1, :, 0:DH],
                                      values[:, b, 0:KT - 1, cols].rearrange("p t (j d) -> p t j d", d=DH)
                                      ).then_inc(values_ready, 1)
                nc.gpsimd.tensor_copy(value_t[i][0:TAIL, KT - 1, :, 0:DH],
                                      values[0:TAIL, b, KT - 1, cols].rearrange("p (j d) -> p j d", d=DH)
                                      ).then_inc(values_ready, 1)

            def negate(b, q):
                u = NQ * b + q
                pool.wait_ge(max_ready, u + 1)
                hold(pool, neg_T, u)
                steps = Chain(pool, neg_step, 4 * u)
                part = [neg_parts[:, :, p, :] for p in range(PARTS)]
                steps.link(nc.gpsimd.tensor_scalar(neg_max[:, :, :], row_max[:, :, :], -1.0, None, ALU.mult))
                steps.link(nc.gpsimd.tensor_copy(part[0], neg_max[:, :, :]))
                steps.link(nc.gpsimd.tensor_tensor(neg_rest[:, :, :], neg_max[:, :, :], part[0], ALU.subtract))
                steps.link(nc.gpsimd.tensor_copy(part[1], neg_rest[:, :, :]))
                nc.gpsimd.tensor_tensor(part[2], neg_rest[:, :, :], part[1], ALU.subtract).then_inc(neg_parts_ready, 1)

            pool.wait_ge(v_by_act, 2 * B)
            pool.wait_ge(v_by_dve, 2 * B)
            load_values(0, 0)
            negate(0, 0)

            def units(b, tail, attn, last):
                for q in range(NQ):
                    u = NQ * b + q
                    if attn and not (last and q == NQ - 1):
                        hold(pool, pv_done, STEPS * u)
                        load_values(*following(b, q))
                    if q == 0 and tail:
                        pool.wait_ge(var_ready, b)
                        steps = Chain(pool, rstd2_step, b - 1)
                        steps.link(nc.gpsimd.tensor_scalar(rstd2[:, :], meanvar2[:, :, 1], EPS, None, ALU.add))
                        nc.gpsimd.tensor_tensor(rstd2[:, :], rstd2[:, :], minus_half[:, 0:QT],
                                                ALU.pow).then_inc(rstd2_ready, 1)
                    if attn and not (last and q == NQ - 1):
                        negate(*following(b, q))

            units(0, False, True, False)
            units(1, True, True, False)
            with pool.Fori(2, B - 1) as b:
                units(b, True, True, False)
            units(B - 1, True, True, True)
            units(B, True, False, True)

        @block.scalar
        def _(act):
            act.wait_ge(ld_w, 16 * 5)
            nc.scalar.activation(gate_t[:, :], gates[:, :], ACT.Tanh).then_inc(gate_step, 1)
            for i in range(2):
                act.wait_ge(xnT_ready, i + 1)
                nc.scalar.copy(xnT[:, i * BANK:(i + 1) * BANK], (up_bank, down_bank)[i][:, :]).then_inc(xnT_copied, 1)

            def cut(i, bank, cols):
                w = cols.stop - cols.start
                act.wait_ge(proj_ready, i + 1)
                nc.scalar.copy(split[:, 0, cols], bank[:, 0:w]).then_inc(hi_ready, 1)
                act.wait_ge(rest_ready, i + 1)
                nc.scalar.copy(split[:, 1, cols], rest[:, i % 2, 0:w]).then_inc(mid_ready, 1)

            for i in range(2):
                cut(i, (pv_bank, misc_bank)[i], slice(i * BANK, (i + 1) * BANK))
            act.wait_ge(q_stored, 16 * PARTS * PARTS)
            for b in range(B):
                if b:
                    act.wait_ge(k_stored, 16 * PARTS * b)
                for c in range(CH):
                    i = 2 + CH * b + c
                    cut(i, (max_bank + score_bank)[c], slice(c * BANK, c * BANK + CW[c]))
                for g in (0, 2):
                    act.wait_ge(v_ready, 4 * b + g + 1)
                    nc.scalar.copy(values[:, b, 4 * g:4 * g + 4, :],
                                   up_bank[:, :].rearrange("p (t n) -> p t n", n=D)).then_inc(v_by_act, 1)

            def exponentials(b, q, s):
                n = NQ * SLOTS * b + SLOTS * q + s
                act.wait_ge(scores_ready, n + 1)
                if s % QH == 0 and s < 2 * QH or s == QH * (STEPS - 1):
                    t = s // QH
                    hold(act, pv_done, STEPS * (NQ * b + q) - (STEPS - 1 - t - (4 if t < 2 else 0)))
                elif s % QH == 0:
                    act.wait_ge(pv_done, STEPS * (NQ * b + q) + s // QH - 1)
                if s < QH * (STEPS - 1):
                    nc.scalar.activation(probs[:, s % (2 * QH), :], score_bank[s % 2][:, :], ACT.Exp,
                                         scale=SCALE).then_inc(probs_ready, 1)
                else:
                    nc.scalar.activation(probs_tail[0:TAIL, s % QH, :], score_bank[s % 2][0:TAIL, :], ACT.Exp,
                                         scale=SCALE).then_inc(probs_ready, 1)

            def neg_copy(b, q):
                act.wait_ge(neg_T, NQ * b + q + 1)
                hold(act, neg_in, 16 * PARTS * (NQ * b + q))
                nc.scalar.copy(neg_rows[:, :], misc_b[0:PARTS * QH, 0:S]).then_inc(neg_rows_ready, 1)

            neg_copy(0, 0)

            def units(b, tail, attn, last):
                for q in range(NQ):
                    u = NQ * b + q
                    for s in range(SLOTS):
                        if attn:
                            exponentials(b, q, s)
                        if s == S_OCOPY and not (q == 0 and not tail) and (attn or q == 0):
                            act.wait_ge(pv_done, STEPS * u)
                            hold(act, out_T, u - 1)
                            nc.scalar.copy(head_outT[:, :], pv_bank[:, 0:S]).then_inc(out_copied, 1)
                        if s == S_MCOPY and attn and not (last and q == NQ - 1):
                            neg_copy(*following(b, q))
                        if tail and q == 0 and s == S_HTCOPY:
                            act.wait_ge(hT_ready, b)
                            nc.scalar.copy(headsT[:, :], up_bank[:, 0:S]).then_inc(hT_copied, 1)
                        if tail and q == 0 and s == S_XNCOPY:
                            act.wait_ge(xn2T_ready, b)
                            nc.scalar.copy(xn2T[:, :], up_bank[:, 0:S]).then_inc(xn2T_copied, 1)
                        if tail and q == 1 and s == 0:
                            act.wait_ge(rel_ready, b)
                            nc.scalar.activation(expo[:, :, :], rel[:, :, :], ACT.Exp).then_inc(expo_ready, 1)
                        if tail:
                            for n, at in expert_tiles(q):
                                if s == at + 1:
                                    g = NT * (b - 1) + n
                                    act.wait_ge(up_ready, g + 1)
                                    hold(act, inner_ready, g - 1)
                                    nc.scalar.activation(th[:, n % 2, :], up_bank[:, 0:S], ACT.Tanh,
                                                         scale=0.5).then_inc(th_ready, 1)

            units(0, False, True, False)
            units(1, True, True, False)
            with act.Fori(2, B - 1) as b:
                units(b, True, True, False)
            units(B - 1, True, True, True)
            units(B, True, False, True)

        @block.vector
        def _(dve):
            nc.vector.memset(keys[NQ - 1][0:PARTS, :, :], 1.0).then_inc(rows_ready, 1)
            dve.wait_ge(ld_x, 16)
            for i in range(B * QT):
                nc.vector.bn_stats(stats[:, i, :], xs[:, i, :]).then_inc(ln_step, 1)
            for i in range(B * QT):
                dve.wait_ge(ln_step, B * QT + i if i else B * QT)
                nc.vector.bn_aggr(meanvar[:, i, :], stats[:, i, :]).then_inc(ln_step, 1)
            dve.wait_ge(rstd_ready, 2)
            for i in range(B * QT):
                nc.vector.tensor_scalar(xn[:, i, :], xs[:, i, :], meanvar[:, i, 0:1], rstd[:, i:i + 1],
                                        ALU.subtract, ALU.mult).then_inc(xn_ready, 1)
            dve.wait_ge(gate_step, 1)
            nc.vector.tensor_scalar(gate_t[:, 1:2], gate_t[:, 1:2], 0.5, None, ALU.mult).then_inc(gates_ready, 1)
            dve.wait_ge(const_ready, 3)
            nc.vector.tensor_copy(iota_f[:, :], iota_i[:, :]).then_inc(gates_ready, 1)

            def masks(g):
                dve.wait_ge(ld_mask, 16 * (QT if g < QT else QT + 3))
                if g < QT:
                    nc.vector.tensor_scalar(masked_q[:, g, :], mask_in[:, g, 0:SK], 0, None,
                                            ALU.is_equal).then_inc(mask_used, 1)
                    return
                n = 7 if g == QT else KT - 1 - 7
                src = mask_in[:, g - QT, 0:n * S].rearrange("p (t q) -> p t q", q=S)
                t0 = 7 * (g - QT)
                nc.vector.tensor_scalar(masked_k[:, t0:t0 + n, :], src, 0, None, ALU.is_equal).then_inc(mask_done, 1)
                if g == QT + 1:
                    nc.vector.tensor_scalar(masked_k[0:TAIL, KT - 1, :], mask_in[0:TAIL, 1, n * S:(n + 1) * S], 0, None,
                                            ALU.is_equal).then_inc(mask_done, 1)

            masks(0)
            masks(1)
            dve.wait_ge(mask_used, 2)
            nc.vector.reduce_max(row_masked[:, :], masked_q[:, :, :], axis=AX.XY).then_inc(mask_done, 1)

            def cut_rest(i, bank, cols):
                w = cols.stop - cols.start
                dve.wait_ge(hi_ready, i + 1)
                hold(dve, lo_ready, i - 1)
                nc.vector.tensor_tensor(rest[:, i % 2, 0:w], bank[:, 0:w], split[:, 0, cols],
                                        ALU.subtract).then_inc(rest_ready, 1)

            for i in range(2):
                cut_rest(i, (pv_bank, misc_bank)[i], slice(i * BANK, (i + 1) * BANK))
            for b in range(B):
                for c in range(CH):
                    cut_rest(2 + CH * b + c, (max_bank + score_bank)[c], slice(c * BANK, c * BANK + CW[c]))
                for g in (1, 3):
                    dve.wait_ge(v_ready, 4 * b + g + 1)
                    if g == 1:
                        nc.vector.tensor_copy(values[:, b, 4 * g:4 * g + 4, :],
                                              down_bank[:, :].rearrange("p (t n) -> p t n", n=D)).then_inc(v_by_dve, 1)
                    else:
                        nc.vector.tensor_copy(values[0:TAIL, b, KT - 1, :], down_bank[0:TAIL, 0:D]).then_inc(v_by_dve, 1)
                if b == 0:
                    dve.wait_ge(flag_sum, 1)
                    nc.vector.tensor_copy(any_masked[:, :], misc_bank[0:1, 0:1]).then_inc(flag_ready, 1)
                    masks(2)
                    masks(3)

            def chunk(b, q, n):
                blk, c = n // CH, n % CH
                j, t = blk // QT, blk % QT
                dve.wait_ge(chunk_ready, NQ * CHUNKS * b + CHUNKS * q + n + 1)
                nc.vector.reduce_max(chunk_max[:, q % 2, t, j, c:c + 1], max_bank[n % 2][:, 0:CW[c]],
                                     axis=AX.X).then_inc(chunk_used, 1)
                if n == CHUNKS - 1:
                    u = NQ * b + q
                    dve.wait_ge(chunk_used, CHUNKS * (u + 1))
                    hold(dve, neg_parts_ready, u)
                    nc.vector.reduce_max(row_max[:, :, :], chunk_max[:, q % 2, :, :, :], axis=AX.X).then_inc(max_ready, 1)

            for n in range(CHUNKS):
                chunk(0, 0, n)
            for n in range(FIRST_CHUNKS):
                chunk(0, 1, n)

            def normalise(u, q):
                dve.wait_ge(out_T, u + 1)
                steps = Chain(dve, out_step, u)
                src = misc_bank[:, 0:S].rearrange("p (t j c) -> p t j c", t=QT, j=QH)
                steps.link(nc.vector.reciprocal(denom[:, :, :], src[:, :, :, DH]))
                if q == 0:
                    hold(dve, hT_ready, u // NQ if isinstance(u, int) else batch_of[0])
                dst = heads[:, :, q * QH * DH:(q + 1) * QH * DH].rearrange("p t (j d) -> p t j d", d=DH)
                nc.vector.tensor_tensor(dst, src[:, :, :, 0:DH], denom[:, :, :, None].broadcast_to([P, QT, QH, DH]),
                                        ALU.mult).then_inc(heads_ready, 1)

            batch_of = [0]

            def residual(b):
                dve.wait_ge(attn_ready, b)
                dve.wait_ge(x_b_in, 16 * b)
                hold(dve, out_stored, 16 * (b - 1))
                steps = Chain(dve, tail_step, 2 * (b - 1))
                steps.link(nc.vector.scalar_tensor_tensor(
                    x1[:, :, :], down_bank[:, 0:S].rearrange("p (t n) -> p t n", n=D), gate_t[:, 0:1], x_b[:, :, :],
                    ALU.mult, ALU.add))
                for t in range(QT):
                    st = nc.vector.bn_stats(stats2[:, t, :], x1[:, t, :])
                steps.link(st)
                for t in range(QT):
                    mv = nc.vector.bn_aggr(meanvar2[:, t, :], stats2[:, t, :])
                mv.then_inc(var_ready, 1)

            def norm2(b):
                dve.wait_ge(rstd2_ready, b)
                for t in range(QT):
                    last = nc.vector.tensor_scalar(xn2[:, t, :], x1[:, t, :], meanvar2[:, t, 0:1], rstd2[:, t:t + 1],
                                                   ALU.subtract, ALU.mult)
                last.then_inc(xn2_ready, 1)

            def top2(b):
                dve.wait_ge(route_ready, b)
                steps = Chain(dve, route_step, 9 * (b - 1))
                steps.link(nc.vector.tensor_copy(logits[:, :, :], down_bank[:, 0:QT * E].rearrange("p (t e) -> p t e", e=E)))
                for t in range(QT):
                    m = nc.vector.max(top[:, t, :], logits[:, t, :])
                steps.link(m)
                for t in range(QT):
                    m = nc.vector.max_index(top_i[:, t, :], top[:, t, :], logits[:, t, :])
                steps.link(m)
                nc.vector.tensor_tensor(rel[:, :, :], logits[:, :, :], top[:, :, 0:1].broadcast_to([P, QT, E]),
                                        ALU.subtract).then_inc(rel_ready, 1)
                steps.link(nc.vector.tensor_copy(top_f[:, :, :], top_i[:, :, :]))

            def weights(b):
                steps = Chain(dve, route_step, 9 * (b - 1) + 4)
                iota = iota_f[:, None, :].broadcast_to([P, QT, E])
                nc.vector.tensor_tensor(first_hot[:, :, :], iota, top_f[:, :, 0:1].broadcast_to([P, QT, E]), ALU.is_equal)
                steps.link(nc.vector.tensor_tensor(second_hot[:, :, :], iota, top_f[:, :, 1:2].broadcast_to([P, QT, E]),
                                                   ALU.is_equal))
                dve.wait_ge(expo_ready, b)
                nc.vector.reduce_sum(total[:, :], expo[:, :, :], axis=AX.X)
                steps.link(nc.vector.tensor_tensor(first_hot[:, :, :], first_hot[:, :, :], second_hot[:, :, :], ALU.add))
                nc.vector.reciprocal(total[:, :], total[:, :])
                steps.link(nc.vector.tensor_tensor(first_hot[:, :, :], first_hot[:, :, :], expo[:, :, :], ALU.mult))
                steps.link(nc.vector.tensor_scalar(total[:, :], total[:, :], gate_t[:, 1:2], None, ALU.mult))
                steps.link(nc.vector.tensor_tensor(combine[:, :, :], first_hot[:, :, :],
                                                   total[:, :, None].broadcast_to([P, QT, E]), ALU.mult))

            def gate_tile(b, n):
                g = NT * (b - 1) + n
                dve.wait_ge(th_ready, g + 1)
                steps = Chain(dve, gated_step, g)
                steps.link(nc.vector.scalar_tensor_tensor(gated[:, :], th[:, n % 2, :], 1.0, up_bank[:, 0:S],
                                                          ALU.add, ALU.mult))
                hold(dve, down_ready, E * (b - 1) + n // TILES - 1)
                nc.vector.tensor_tensor(inner[:, n % 4, :], gated[:, :], up_bank[:, S:2 * S], ALU.mult).then_inc(inner_ready, 1)

            def add_expert(b, e):
                g = E * (b - 1) + e
                dve.wait_ge(down_ready, g + 1)
                hold(dve, down_used, g)
                for t in range(QT):
                    last = nc.vector.scalar_tensor_tensor(x1[:, t, :], down_bank[:, t * D:(t + 1) * D],
                                                          combine[:, t, e:e + 1], x1[:, t, :], ALU.mult, ALU.add)
                last.then_inc(down_used, 1)

            def units(b, tail, attn, last):
                for q in range(NQ):
                    u = NQ * b + q
                    for s in range(SLOTS):
                        if attn:
                            for n in max_chunks(s):
                                by, m = (1, n) if n < CHUNKS else (2, n - CHUNKS)
                                if not (last and q + by >= NQ):
                                    chunk(*following(b, q, by), m)
                        if s == S_ONORM and not (q == 0 and not tail) and (attn or q == 0):
                            batch_of[0] = b
                            normalise(u - 1, (q - 1) % NQ)
                        if tail and q == 0:
                            if s == S_X1:
                                residual(b)
                            if s == S_XN:
                                norm2(b)
                            if s == S_TOP:
                                top2(b)
                        if tail and q == 1 and s == 1:
                            weights(b)
                        if tail:
                            for n, at in expert_tiles(q):
                                if s == at + 2:
                                    gate_tile(b, n)
                                if s == min(at + 5, SLOTS - 1) and n % TILES == TILES - 1:
                                    add_expert(b, n // TILES)

            units(0, False, True, False)
            units(1, True, True, False)
            with dve.Fori(2, B - 1) as b:
                units(b, True, True, False)
            units(B - 1, True, True, True)
            units(B, True, False, True)

        @block.tensor
        def _(pe):
            pe.wait_ge(ident_ready, 3)
            for i in range(B * QT):
                pe.wait_ge(xn_ready, i + 1)
                bank = (up_bank, down_bank)[i // 4]
                last = nc.tensor.transpose(bank[:, (i % 4) * P:(i % 4 + 1) * P], xn[:, i, :], ident[:, :])
                if i % 4 == 3:
                    last.then_inc(xnT_ready, 1)
            pe.wait_ge(ld_w, 16 * 5)
            for i in range(2):
                pe.wait_ge(xnT_copied, i + 1)
                nc.tensor.matmul((pv_bank, misc_bank)[i][:, :], wq[:, :], xnT[:, i * BANK:(i + 1) * BANK],
                                 start=True, stop=True).then_inc(proj_ready, 1)
            for b in range(B):
                pe.wait_ge(ld_ctx[b % 2], 16 * (b // 2 + 1))
                for c in range(CH):
                    i = 2 + CH * b + c
                    if b:
                        pe.wait_ge(rest_ready, i - CH + 1)
                    nc.tensor.matmul((max_bank + score_bank)[c][:, 0:CW[c]], wk[:, :],
                                     ctx_in[:, b % 2, c * BANK:c * BANK + CW[c]], start=True, stop=True).then_inc(proj_ready, 1)
                for g in range(4):
                    if b or g >= 2:
                        pe.wait_ge(v_by_dve if g % 2 else v_by_act, 2 * b + g // 2)
                    for t in range(4 * g, min(4 * g + 4, KT)):
                        w = P if t < KT - 1 else TAIL
                        last = nc.tensor.matmul((up_bank, down_bank)[1 if g == 3 else g % 2][0:w, (t % 4) * D:(t % 4 + 1) * D],
                                                ctx_in[:, b % 2, t * P:t * P + w], wv[:, :], start=True, stop=True)
                    last.then_inc(v_ready, 1)
                if b == 0:
                    pe.wait_ge(mask_done, 1)
                    pe.wait_ge(const_ready, 1)
                    pe.wait_ge(rest_ready, 2)
                    nc.tensor.matmul(misc_bank[0:1, 0:1], row_masked[:, :], ones_col[:, :],
                                     start=True, stop=True).then_inc(flag_sum, 1)
            pe.wait_ge(v_by_act, 2 * B)
            pe.wait_ge(v_by_dve, 2 * B)
            pe.wait_ge(rest_ready, 2 + CH * B)
            pe.wait_ge(mask_done, 4)
            pe.wait_ge(ld_fw, 16 * 4)
            pe.wait_ge(flag_ready, 1)
            masked = pe.value_load(any_masked[0:1, 0:1], min_val=0, max_val=P)

            def attention(with_mask):

                def chunk(b, q, n):
                    blk, c = n // CH, n % CH
                    j, t = blk // QT, blk % QT
                    if n == 0:
                        pe.wait_ge(ld_unit[q], 16 * (PARTS + 1) * (b + 1))
                    hold(pe, chunk_used, NQ * CHUNKS * b + CHUNKS * q + n - 1)
                    dst = max_bank[n % 2][:, 0:CW[c]]
                    last = nc.tensor.matmul(dst, queries[q][0:ROWS, j, t * P:(t + 1) * P],
                                            keys[q][0:ROWS, j, c * BANK:c * BANK + CW[c]], start=True, stop=not with_mask)
                    if with_mask:
                        last = nc.tensor.matmul(dst, ident_neg[:, :], masked_q[:, t, c * BANK:c * BANK + CW[c]],
                                                start=False, stop=True)
                    last.then_inc(chunk_ready, 1)

                def scores(b, q, s):
                    if s == 0:
                        pe.wait_ge(neg_in, 16 * PARTS * (NQ * b + q + 1))
                    hold(pe, probs_ready, NQ * SLOTS * b + SLOTS * q + s - 1)
                    for i in range(2):
                        j, t = (s % QH, 2 * (s // QH) + i) if s < QH * (STEPS - 1) else (2 * (s % QH) + i, KT - 1)
                        w = P if t < KT - 1 else TAIL
                        dst = score_bank[s % 2][0:w, i * S:(i + 1) * S]
                        last = nc.tensor.matmul(dst, keys[q][0:KR, j, t * P:t * P + w], queries[q][0:KR, j, :],
                                                start=True, stop=not with_mask)
                        if with_mask:
                            last = nc.tensor.matmul(dst, ident_neg[0:w, 0:w], masked_k[0:w, t, :], start=False, stop=True)
                    last.then_inc(scores_ready, 1)

                def probs_v(u, q, t):
                    pe.wait_ge(probs_ready, SLOTS * u + min(QH * (t + 1), SLOTS))
                    if t == 0:
                        pe.wait_ge(values_ready, 2 * (u + 1))
                        hold(pe, out_copied, u)
                    for i in range(2 if t < STEPS - 1 else 1):
                        kt = 2 * t + i
                        w = P if kt < KT - 1 else TAIL
                        for j in range(QH):
                            if kt < KT - 1:
                                p = probs[:, QH * (t % 2) + j, i * S:(i + 1) * S]
                            else:
                                p = probs_tail[0:w, j // 2, (j % 2) * S:(j % 2 + 1) * S]
                            last = nc.tensor.matmul(pv_bank[VW * j:VW * (j + 1), 0:S], value_t[q % 2][0:w, kt, j, :], p,
                                                    start=kt == 0, stop=kt == KT - 1)
                    last.then_inc(pv_done, 1)

                def neg_transpose(b, q):
                    u = NQ * b + q
                    pe.wait_ge(neg_parts_ready, u + 1)
                    hold(pe, heads_ready, u - 1)
                    hold(pe, neg_rows_ready, u)
                    for t in range(QT):
                        last = nc.tensor.transpose(misc_b[0:PARTS * QH, t * P:(t + 1) * P],
                                                   neg_parts[:, t, :, :].rearrange("p c j -> p (c j)"), ident_b[:, :])
                    last.then_inc(neg_T, 1)

                def expert_up(b, n):
                    e, i = n // TILES, n % TILES
                    hold(pe, inner_ready, NT * (b - 1) + n)
                    if n == 0:
                        pe.wait_ge(xn2T_copied, b)
                    for k in range(2):
                        last = nc.tensor.matmul(up_bank[:, k * S:(k + 1) * S], w1[:, e, k * INTER + i * P:k * INTER + (i + 1) * P],
                                                xn2T[:, :], start=True, stop=True)
                    last.then_inc(up_ready, 1)

                def expert_down(b, e):
                    pe.wait_ge(inner_ready, NT * (b - 1) + TILES * (e + 1))
                    hold(pe, down_used, E * (b - 1) + e)
                    if e == 0:
                        pe.wait_ge(rel_ready, b)
                    for t in range(QT):
                        for i in range(TILES):
                            last = nc.tensor.matmul(down_bank[:, t * D:(t + 1) * D],
                                                    inner[:, (TILES * e + i) % 4, t * P:(t + 1) * P], w2[:, e, i, :],
                                                    start=i == 0, stop=i == TILES - 1)
                    last.then_inc(down_ready, 1)

                def tail_slot(b, s):
                    if s == S_HT:
                        pe.wait_ge(heads_ready, NQ * b)
                        hold(pe, inner_ready, NT * (b - 1))
                        for t in range(QT):
                            last = nc.tensor.transpose(up_bank[:, t * P:(t + 1) * P], heads[:, t, :], ident[:, :])
                        last.then_inc(hT_ready, 1)
                    if s == S_PROJ:
                        pe.wait_ge(hT_copied, b)
                        hold(pe, down_used, E * (b - 1))
                        for t in range(QT):
                            last = nc.tensor.matmul(down_bank[:, t * D:(t + 1) * D], headsT[:, t * P:(t + 1) * P], wt[:, :],
                                                    start=True, stop=True)
                        last.then_inc(attn_ready, 1)
                    if s == S_XNTR:
                        pe.wait_ge(xn2_ready, b)
                        for t in range(QT):
                            last = nc.tensor.transpose(up_bank[:, t * P:(t + 1) * P], xn2[:, t, :], ident[:, :])
                        last.then_inc(xn2T_ready, 1)
                    if s == S_ROUTE:
                        pe.wait_ge(xn2T_copied, b)
                        for t in range(QT):
                            last = nc.tensor.matmul(down_bank[:, t * E:(t + 1) * E], xn2T[:, t * P:(t + 1) * P], wr[:, :],
                                                    start=True, stop=True)
                        last.then_inc(route_ready, 1)

                def units(b, tail, attn, last):
                    for q in range(NQ):
                        u = NQ * b + q
                        for s in range(SLOTS):
                            before = not (q == 0 and not tail) and (attn or q == 0)
                            if attn:
                                scores(b, q, s)
                                for n in max_chunks(s):
                                    by, m = (1, n) if n < CHUNKS else (2, n - CHUNKS)
                                    if not (last and q + by >= NQ):
                                        chunk(*following(b, q, by), m)
                            if s == S_PVTAIL and before:
                                probs_v(u - 1, (q - 1) % NQ, STEPS - 1)
                            if attn and s % QH == 1 and s > QH:
                                probs_v(u, q, s // QH - 1)
                            if s == S_OTR and before:
                                pe.wait_ge(out_copied, u)
                                hold(pe, neg_rows_ready, u + 1 if attn else u)
                                for t in range(QT):
                                    tr = nc.tensor.transpose(misc_bank[:, t * P:(t + 1) * P],
                                                             head_outT[:, t * P:(t + 1) * P], ident[:, :])
                                tr.then_inc(out_T, 1)
                            if s == S_MTR and attn and not (last and q == NQ - 1):
                                neg_transpose(*following(b, q))
                            if tail and q == 0:
                                tail_slot(b, s)
                            if tail:
                                for n, at in expert_tiles(q):
                                    if s == at:
                                        expert_up(b, n)
                                    if s == at + 3 and n % TILES == TILES - 1:
                                        expert_down(b, n // TILES)

                for n in range(CHUNKS):
                    chunk(0, 0, n)
                for n in range(FIRST_CHUNKS):
                    chunk(0, 1, n)
                neg_transpose(0, 0)
                units(0, False, True, False)
                units(1, True, True, False)
                with pe.Fori(2, B - 1) as b:
                    units(b, True, True, False)
                units(B - 1, True, True, True)
                units(B, True, False, True)

            with pe.If(masked != 0):
                attention(True)
            with pe.Else():
                attention(False)


def kernel(**inputs):
    import concourse.bacc as bacc
    from concourse.bass_utils import run_bass_kernel_spmd

    a = {k: np.asarray(v) for k, v in inputs.items()}
    mask = a["mask_1x1xSxS2_if1"][0, 0]
    arrays = {
        "x": a["x"],
        "ctxT": a["ctx_1024"].transpose(0, 2, 1),
        "mask": mask,
        "maskT": mask.T,
        "g_x": a["g_xattn"],
        "g_f": a["g_ffn"],
        "W_Q": a["L0_xattn_W_Q"],
        "W_K": a["L0_xattn_W_K"],
        "W_V": a["L0_xattn_W_V"],
        "W_T": a["L0_xattn_W_T"],
        "w1T": a["L0_ffn_w1"].reshape(E * 2 * INTER, D).T,
        "w2T": a["L0_ffn_w2"].transpose(0, 2, 1),
        "rT": a["L0_ffn_router_w"].T,
    }
    arrays = {k: np.ascontiguousarray(v) for k, v in arrays.items()}
    nc = bacc.Bacc("TRN2", target_bir_lowering=False, num_devices=1)
    args = [nc.dram_tensor(k, v.shape, mybir.dt.from_np(v.dtype), kind="ExternalInput").ap() for k, v in arrays.items()]
    out = nc.dram_tensor("out", (B, S, D), FP32, kind="ExternalOutput").ap()
    block_kernel(nc, *args, out)
    r = run_bass_kernel_spmd(nc, [arrays], core_ids=[0])
    return r.results[0]["out"]
```

```python
from contextlib import ExitStack

import numpy as np

import concourse.bass as bass
from concourse import mybir

FP32, BF16 = mybir.dt.float32, mybir.dt.bfloat16
I32, U32 = mybir.dt.int32, mybir.dt.uint32
ALU, ACT, AX = mybir.AluOpType, mybir.ActivationFunctionType, mybir.AxisListType

P = 128
B, S, D = 4, 256, 128
SK = 1601
H, DH = 16, 8
E, INTER = 8, 256
QH = 4
NQ = H // QH
QT = S // P
KT = -(-SK // P)
TAIL = SK - (KT - 1) * P
PARTS = 3
ROWS = PARTS * PARTS * DH
NEG = ROWS
KR = ROWS + PARTS
BANK = 512
CH = -(-SK // BANK)
CW = [min(BANK, SK - c * BANK) for c in range(CH)]
HALF = QH * QT // 2
MAXB = 3
CHUNKS = 2 * (HALF * (CH - 1) + 1)
STEPS = (KT + 1) // 2
SLOTS = QH * (STEPS - 1) + QH // 2
LEAD = 9
TILES = INTER // P
NT = E * TILES
VW = 32
EPS = 1e-5
MASKED = -float(2 ** 100)
SCALE = 1.0 / float(np.sqrt(DH))

S_OCOPY, S_OTR, S_ONORM = 3, 5, 6
S_MTR, S_MCOPY = 19, 20
S_HT, S_HTCOPY, S_PROJ, S_X1, S_XN, S_XNTR, S_XNCOPY, S_ROUTE, S_TOP = 9, 11, 13, 14, 16, 18, 20, 22, 24
TILE_AT = [2 + n * ((NQ - 1) * SLOTS - 7) // NT for n in range(NT)]
DOWN_AFTER = 5
assert not {(at + DOWN_AFTER) % SLOTS for at in TILE_AT[TILES - 1::TILES]} & {S_OTR, S_MTR}


def hold(eng, sem, n):
    if not isinstance(n, int) or n > 0:
        eng.wait_ge(sem, n)


class Chain:

    def __init__(self, eng, sem, start=0):
        self.eng, self.sem, self.n = eng, sem, start

    def link(self, ins):
        ins.then_inc(self.sem, 1)
        self.n = self.n + 1
        self.eng.wait_ge(self.sem, self.n)


def following(b, q, by=1):
    return (b + (q + by) // NQ, (q + by) % NQ)


def score_rows(n):
    half, i = divmod(n, CHUNKS // 2)
    if i < HALF * (CH - 1):
        return [(half * HALF + i // (CH - 1), i % (CH - 1))]
    return [(half * HALF + r, CH - 1) for r in range(HALF)]


def bank_free(n):
    return MAXB if n >= MAXB else next(CHUNKS + n - m for m in reversed(range(CHUNKS)) if m % MAXB == n)


def expert_work(q, s, after=0):
    return [n for n in range(NT) if TILE_AT[n] + after == (q - 1) * SLOTS + s]


def experts_done(q, s):
    return sum(TILE_AT[TILES * e + TILES - 1] + DOWN_AFTER < (q - 1) * SLOTS + s for e in range(E))


def value_tiles(s):
    at = [QH * (t // 2) + QH + 1 + 2 * (t % 2) for t in range(KT - 1)] + [SLOTS + 2]
    return [(at[t] // SLOTS, t) for t in range(KT) if at[t] % SLOTS == s]


def block_kernel(nc, x, ctxT, mask, maskT, g_x, g_f, W_Q, W_K, W_V, W_T, w1T, w2T, rT, out):
    es = ExitStack()
    sb = lambda name, shape, dt: es.enter_context(nc.sbuf_tensor(name, shape, dt))
    ps = lambda name, dt=FP32: es.enter_context(nc.psum_tensor(name, [P, BANK * 4 // (2 if dt == BF16 else 4)], dt))
    sem = lambda name: es.enter_context(nc.semaphore(name))

    with es:
        k_parts_dram = nc.dram_tensor("k_parts", [B, H, PARTS, DH, SK], BF16).ap()
        q_parts_dram = nc.dram_tensor("q_parts", [H, PARTS, PARTS, DH, B * S], BF16).ap()

        wq, wk, wv, wt = (sb(n, [P, D], FP32) for n in ("wq", "wk", "wv", "wt"))
        w2 = sb("w2", [P, E, TILES, D], FP32)
        wr = sb("wr", [P, E], FP32)
        gates = sb("gates", [P, 2], FP32)
        gate_t = sb("gate_t", [P, 2], FP32)
        ctx_in = sb("ctx_in", [P, 2, SK], FP32)
        masked_q = sb("masked_q", [P, QT, SK], BF16)
        masked_k = sb("masked_k", [P, KT, S], BF16)
        row_masked = sb("row_masked", [P, 1], FP32)
        any_masked = sb("any_masked", [1, 1], I32)
        ident = sb("ident", [P, P], FP32)
        ident_b = sb("ident_b", [P, P], BF16)
        ident_neg = sb("ident_neg", [P, P], BF16)
        ones_col = sb("ones_col", [P, 1], FP32)
        iota_i = sb("iota_i", [P, E], I32)
        iota_f = sb("iota_f", [P, E], FP32)
        minus_half = sb("minus_half", [P, B * QT], FP32)
        xs = sb("xs", [P, B * QT, D], FP32)
        stats = sb("stats", [P, B * QT, 6], FP32)
        meanvar = sb("meanvar", [P, B * QT, 2], FP32)
        rstd = sb("rstd", [P, B * QT], FP32)
        split0 = sb("split0", [P, PARTS, SK], BF16)
        rest = sb("rest", [P, 2, BANK], FP32)
        keys = [sb(f"keys{i}", [P, QH, SK], BF16) for i in range(NQ)]
        queries = [sb(f"queries{i}", [P, QH, S], BF16) for i in range(NQ)]
        values = sb("values", [P, B, KT, D], FP32)
        value_t = [sb(f"value_t{i}", [P, KT, QH, VW], FP32) for i in range(2)]
        probs = sb("probs", [P, 2 * QH, 2 * S], FP32)
        probs_tail = sb("probs_tail", [P, QH // 2, 2 * S], FP32)
        chunk_max = sb("chunk_max", [P, 2, QT, QH, CH], FP32)
        row_max = sb("row_max", [P, QT, QH], FP32)
        neg_max = sb("neg_max", [P, QT, QH], FP32)
        neg_rest = sb("neg_rest", [P, QT, QH], FP32)
        neg_parts = sb("neg_parts", [P, QT, PARTS, QH], BF16)
        neg_rows = sb("neg_rows", [PARTS * QH, S], BF16)
        head_outT = sb("head_outT", [P, S], FP32)
        denom = sb("denom", [P, QT, QH], FP32)
        heads = sb("heads", [P, QT, D], FP32)
        x1 = sb("x1", [P, QT, D], FP32)
        stats2 = sb("stats2", [P, QT, 6], FP32)
        meanvar2 = sb("meanvar2", [P, QT, 2], FP32)
        rstd2 = sb("rstd2", [P, QT], FP32)
        logits = sb("logits", [P, QT, E], FP32)
        top = sb("top", [P, QT, 8], FP32)
        top_i = sb("top_i", [P, QT, 8], U32)
        top_f = sb("top_f", [P, QT, 8], FP32)
        rel = sb("rel", [P, QT, E], FP32)
        expo = sb("expo", [P, QT, E], FP32)
        first_hot = sb("first_hot", [P, QT, E], FP32)
        second_hot = sb("second_hot", [P, QT, E], FP32)
        total = sb("total", [P, QT], FP32)
        combine = sb("combine", [P, QT, E], FP32)
        w1 = sb("w1", [P, E, 2 * INTER], FP32)
        late = sb("late", [P, 12 * S], FP32)
        headsT, xn2T, gated0, gated1 = (late[:, i * S:(i + 1) * S] for i in (0, 1, 2, 11))
        x_b, xn2 = (late[:, i * S:(i + 1) * S].rearrange("p (t d) -> p t d", d=D) for i in (3, 4))
        th = late[:, 5 * S:7 * S].rearrange("p (n s) -> p n s", s=S)
        inner = late[:, 7 * S:11 * S].rearrange("p (n s) -> p n s", s=S)
        mask_in = w1[:, :, :].rearrange("p e i -> p (e i)").bitcast(I32).rearrange("p (g k) -> p g k", g=2)
        spare = probs[:, :, :].rearrange("p a b -> p (a b)")
        xn = spare[:, 0:B * S].rearrange("p (t d) -> p t d", d=D)
        xnT = spare[:, B * S:2 * B * S]
        q_split = spare[:, 2 * B * S:4 * B * S].bitcast(BF16)[:, 0:PARTS * B * S].rearrange("p (c t) -> p c t", c=PARTS)
        split1 = late[:, :].bitcast(BF16)[:, 0:PARTS * SK].rearrange("p (c k) -> p c k", c=PARTS)
        splits = [split0, split1]

        max_bank = [ps(f"max_bank{i}") for i in range(MAXB)]
        score_bank = [ps("score_bank0"), ps("score_bank1")]
        pv_bank = ps("pv_bank")
        up_bank = ps("up_bank")
        down_bank = ps("down_bank")
        down_b = down_bank[:, :].bitcast(BF16)
        cuts = [(0, c) for c in range(CH)] + [(None, c) for c in range(2)] + [(b, c) for b in range(1, B) for c in range(CH)]
        cut_banks = score_bank + [pv_bank]
        cuts = [(b, c, cut_banks[i % 3], q_split if b is None else splits[b % 2],
                 slice(c * BANK, c * BANK + (BANK if b is None else CW[c]))) for i, (b, c) in enumerate(cuts)]
        last_cut = [max(i for i, x in enumerate(cuts) if x[0] == b) for b in range(B)]
        last_q_cut = max(i for i, x in enumerate(cuts) if x[0] is None)
        pieces = [piece for b in range(2, B) for piece in
                  [("K", last_cut[b] - (CH - 1) + c) for c in range(CH)] + [("V", (b, g)) for g in range(4)]]
        up_banks, down_banks = [up_bank] + score_bank, [down_bank] + max_bank
        early = [(0, 0, n) for n in range(CHUNKS)] + [(0, 1, n) for n in range(LEAD)]

        ld_x, ld_wk, ld_wv, ld_w, ld_fw, ld_mask = (
            sem("ld_x"), sem("ld_wk"), sem("ld_wv"), sem("ld_w"), sem("ld_fw"), sem("ld_mask"))
        ld_ctx = [sem("ld_ctx0"), sem("ld_ctx1")]
        const_ready, ident_ready, neg_ready = sem("const_ready"), sem("ident_ready"), sem("neg_ready")
        zeroed = sem("zeroed")
        rows_ready = sem("rows_ready")
        ln_step, rstd_ready, xn_ready = sem("ln_step"), sem("rstd_ready"), sem("xn_ready")
        xnT_ready, xnT_copied = sem("xnT_ready"), sem("xnT_copied")
        proj_ready, hi_ready, rest_ready, mid_ready, lo_ready = (
            sem("proj_ready"), sem("hi_ready"), sem("rest_ready"), sem("mid_ready"), sem("lo_ready"))
        v_ready, v_by_act, v_by_dve = sem("v_ready"), sem("v_by_act"), sem("v_by_dve")
        q_stored, k_stored, ones_rows = sem("q_stored"), [sem(f"k_stored{i}") for i in range(2)], sem("ones_rows")
        q_rest_stored, ld_maskT = sem("q_rest_stored"), sem("ld_maskT")
        mask_used, mask_done, flag_sum, flag_ready = (
            sem("mask_used"), sem("mask_done"), sem("flag_sum"), sem("flag_ready"))
        gate_step, gates_ready = sem("gate_step"), sem("gates_ready")
        ld_unit = [sem(f"ld_unit{i}") for i in range(NQ)]
        chunk_ready, chunk_used = sem("chunk_ready"), sem("chunk_used")
        max_ready, neg_step, neg_parts_ready = sem("max_ready"), sem("neg_step"), sem("neg_parts_ready")
        neg_T, neg_rows_ready, neg_in = sem("neg_T"), sem("neg_rows_ready"), sem("neg_in")
        scores_ready, probs_ready, pv_done = sem("scores_ready"), sem("probs_ready"), sem("pv_done")
        values_ready = sem("values_ready")
        out_copied, out_T, out_step, heads_ready = sem("out_copied"), sem("out_T"), sem("out_step"), sem("heads_ready")
        hT_ready, hT_copied, attn_ready = sem("hT_ready"), sem("hT_copied"), sem("attn_ready")
        x_b_in, tail_step, var_ready, rstd2_ready, xn2_ready = (
            sem("x_b_in"), sem("tail_step"), sem("var_ready"), sem("rstd2_ready"), sem("xn2_ready"))
        rstd2_step = sem("rstd2_step")
        xn2T_ready, xn2T_copied, route_ready = sem("xn2T_ready"), sem("xn2T_copied"), sem("route_ready")
        rel_ready, expo_ready, route_step = sem("rel_ready"), sem("expo_ready"), sem("route_step")
        up_ready, th_ready, gated_step, inner_ready = sem("up_ready"), sem("th_ready"), sem("gated_step"), sem("inner_ready")
        down_ready, down_used, out_stored = sem("down_ready"), sem("down_used"), sem("out_stored")

        block = es.enter_context(nc.Block())

        @block.sync
        def _(sp):
            x_rows = x.rearrange("b (t p) d -> p (b t) d", p=P)
            out_rows = out.rearrange("b (t p) d -> b p t d", p=P)

            def load_ctx(b):
                if b >= 2:
                    sp.wait_ge(proj_ready, last_cut[b - 2] + 1)
                    sp.wait_ge(v_ready, 4 * (b - 1))
                sp.dma_start(ctx_in[:, b % 2, :], ctxT[b]).then_inc(ld_ctx[b % 2], 16)

            def load_unit(b, q):
                h0 = QH * q
                for c in range(PARTS):
                    rows = slice(c * PARTS * DH, (c + 1) * PARTS * DH)
                    sp.dma_start(keys[q][rows, :, :],
                                 k_parts_dram[b, h0:h0 + QH].rearrange("j p d k -> (p d) j k")).then_inc(ld_unit[q], 16)
                sp.dma_start(queries[q][0:ROWS, :, :],
                             q_parts_dram[h0:h0 + QH, :, :, :, bass.ds(b * S, S)].rearrange("j c p d t -> (c p d) j t")
                             ).then_inc(ld_unit[q], 16)

            def load_neg(b, q):
                sp.wait_ge(neg_rows_ready, NQ * b + q + 1)
                for p in range(PARTS):
                    sp.dma_start(queries[q][NEG + p:NEG + p + 1, :, :], neg_rows[p * QH:(p + 1) * QH, :]).then_inc(neg_in, 16)

            def store_keys(b):
                sp.wait_ge(lo_ready, last_cut[b] + 1)
                for p in range(PARTS):
                    sp.dma_start(k_parts_dram[b, :, p], splits[b % 2][:, p, :]).then_inc(k_stored[b % 2], 16)

            sp.dma_start(xs[:, :, :], x_rows).then_inc(ld_x, 16)
            sp.dma_start(wk[:, :], W_K).then_inc(ld_wk, 16)
            load_ctx(0)
            sp.dma_start(wq[:, :], W_Q).then_inc(ld_w, 16)
            sp.dma_start(gates[:, 0:1], g_x.rearrange("(o g) -> o g", o=1).broadcast_to([P, 1])).then_inc(ld_w, 16)
            sp.dma_start(gates[:, 1:2], g_f.rearrange("(o g) -> o g", o=1).broadcast_to([P, 1])).then_inc(ld_w, 16)
            sp.dma_start(wv[:, :], W_V).then_inc(ld_wv, 16)
            for t in range(QT):
                sp.dma_start(mask_in[:, t, 0:SK], mask.rearrange("(t p) k -> p t k", p=P)[:, t, :]).then_inc(ld_mask, 16)
            sp.wait_ge(rows_ready, 1)
            for i in range(NQ):
                sp.dma_start(keys[i][NEG:KR, :, :], keys[NQ - 1][0:PARTS, :, :]).then_inc(ones_rows, 16)
            load_ctx(1)
            store_keys(0)
            sp.wait_ge(lo_ready, last_q_cut + 1)
            for tokens in (slice(0, S), slice(S, B * S)):
                for c in range(PARTS):
                    for p in range(PARTS):
                        sp.dma_start(q_parts_dram[:, c, p, :, tokens], q_split[:, c, tokens]).then_inc(
                            q_stored if tokens.start == 0 else q_rest_stored, 16)
                if tokens.start == 0:
                    sp.wait_ge(ones_rows, 16 * NQ)
                    sp.wait_ge(k_stored[0], 16 * PARTS)
                    sp.wait_ge(q_stored, 16 * PARTS * PARTS)
                    load_unit(0, 0)
                    load_unit(0, 1)
                    load_ctx(2)
            store_keys(1)
            load_ctx(3)
            store_keys(2)
            store_keys(3)
            load_neg(0, 0)
            sp.wait_ge(mask_done, 4)
            sp.dma_start(w1[:, :, :], w1T.rearrange("d (e i) -> d e i", e=E)).then_inc(ld_fw, 16)
            sp.dma_start(w2[:, :, :, :], w2T.rearrange("e (t p) h -> p e t h", p=P)).then_inc(ld_fw, 16)
            sp.dma_start(wt[:, :], W_T).then_inc(ld_fw, 16)
            sp.dma_start(wr[:, :], rT).then_inc(ld_fw, 16)
            sp.wait_ge(q_rest_stored, 16 * PARTS * PARTS)
            sp.wait_ge(k_stored[0], 16 * PARTS * 2)
            sp.wait_ge(k_stored[1], 16 * PARTS * 2)

            def units(b, tail, attn, last):
                for q in range(NQ):
                    u = NQ * b + q
                    if q == 0 and tail:
                        if not isinstance(b, int) or b >= 2:
                            sp.wait_ge(down_used, E * (b - 1))
                            sp.dma_start(out_rows[b - 2], x1[:, :, :]).then_inc(out_stored, 16)
                        hold(sp, var_ready, b - 1)
                        sp.dma_start(x_b[:, :, :], x[b - 1].rearrange("(t p) d -> p t d", p=P)).then_inc(x_b_in, 16)
                    if not attn:
                        continue
                    if not (last and q >= NQ - 2):
                        hold(sp, scores_ready, SLOTS * (u - 1))
                        load_unit(*following(b, q, 2))
                    if not (last and q == NQ - 1):
                        load_neg(*following(b, q))

            units(0, False, True, False)
            units(1, True, True, False)
            with sp.Fori(2, B - 1) as b:
                units(b, True, True, False)
            units(B - 1, True, True, True)
            units(B, True, False, True)
            sp.wait_ge(down_used, E * B)
            sp.dma_start(out_rows[B - 1], x1[:, :, :]).then_inc(out_stored, 16)
            sp.wait_ge(out_stored, 16 * B)

        @block.gpsimd
        def _(pool):
            nc.gpsimd.memset(keys[NQ - 1][0:PARTS, :, :], 1.0).then_inc(rows_ready, 1)
            nc.gpsimd.memset(ident[:, :], 0.0).then_inc(zeroed, 1)
            nc.gpsimd.memset(ident_b[:, :], 0.0).then_inc(zeroed, 1)
            nc.gpsimd.memset(ident_neg[:, :], 0.0).then_inc(zeroed, 1)
            pool.wait_ge(zeroed, 3)
            for m, fill in ((ident, 1.0), (ident_b, 1.0), (ident_neg, MASKED)):
                nc.gpsimd.affine_select(out=m[:, :], in_=m[:, :], compare_op=ALU.not_equal, fill=fill, base=0,
                                        pattern=[[-1, P]], channel_multiplier=1).then_inc(ident_ready, 1)
            nc.gpsimd.memset(ones_col[:, :], 1.0).then_inc(const_ready, 1)
            nc.gpsimd.memset(minus_half[:, :], -0.5).then_inc(const_ready, 1)
            nc.gpsimd.iota(iota_i[:, :], pattern=[[1, E]], base=0, channel_multiplier=0).then_inc(const_ready, 1)
            for i in range(2):
                nc.gpsimd.memset(value_t[i][:, :, :, :], 0.0).then_inc(const_ready, 1)
            pool.wait_ge(const_ready, 5)
            for i in range(2):
                nc.gpsimd.memset(value_t[i][:, :, :, DH:DH + 1], 1.0).then_inc(const_ready, 1)
            def third_part(i):
                _, _, _, parts, cols = cuts[i]
                pool.wait_ge(mid_ready, i + 1)
                nc.gpsimd.tensor_tensor(parts[:, 2, cols], rest[:, i % 2, 0:cols.stop - cols.start], parts[:, 1, cols],
                                        ALU.subtract).then_inc(lo_ready, 1)

            pool.wait_ge(ln_step, 2 * B * QT)
            chain = Chain(pool, rstd_ready)
            chain.link(nc.gpsimd.tensor_scalar(rstd[:, :], meanvar[:, :, 1], EPS, None, ALU.add))
            nc.gpsimd.tensor_tensor(rstd[:, :], rstd[:, :], minus_half[:, :], ALU.pow).then_inc(rstd_ready, 1)
            for i in range(len(cuts)):
                third_part(i)
                if i == last_cut[1]:
                    for g in range(2):
                        pool.wait_ge(mask_used, g + 1)
                        n = 7 if g == 0 else KT - 1 - 7
                        pool.dma_start(mask_in[:, g, 0:n * S].rearrange("p (t q) -> p t q", q=S),
                                       maskT[g * 7 * P:(g * 7 + n) * P, :].rearrange("(t p) q -> p t q", p=P)
                                       ).then_inc(ld_maskT, 16)
                    pool.dma_start(mask_in[0:TAIL, 1, (KT - 8) * S:(KT - 7) * S], maskT[(KT - 1) * P:SK, :]).then_inc(ld_maskT, 16)

            def load_values(b, q):
                i, cols = q % 2, slice(q * QH * DH, (q + 1) * QH * DH)
                nc.gpsimd.tensor_copy(value_t[i][:, 0:KT - 1, :, 0:DH],
                                      values[:, b, 0:KT - 1, cols].rearrange("p t (j d) -> p t j d", d=DH)
                                      ).then_inc(values_ready, 1)
                nc.gpsimd.tensor_copy(value_t[i][0:TAIL, KT - 1, :, 0:DH],
                                      values[0:TAIL, b, KT - 1, cols].rearrange("p (j d) -> p j d", d=DH)
                                      ).then_inc(values_ready, 1)

            def negate(b, q):
                u = NQ * b + q
                pool.wait_ge(max_ready, u + 1)
                hold(pool, neg_T, u)
                steps = Chain(pool, neg_step, 4 * u)
                part = [neg_parts[:, :, p, :] for p in range(PARTS)]
                steps.link(nc.gpsimd.tensor_scalar(neg_max[:, :, :], row_max[:, :, :], -1.0, None, ALU.mult))
                steps.link(nc.gpsimd.tensor_copy(part[0], neg_max[:, :, :]))
                steps.link(nc.gpsimd.tensor_tensor(neg_rest[:, :, :], neg_max[:, :, :], part[0], ALU.subtract))
                steps.link(nc.gpsimd.tensor_copy(part[1], neg_rest[:, :, :]))
                nc.gpsimd.tensor_tensor(part[2], neg_rest[:, :, :], part[1], ALU.subtract).then_inc(neg_parts_ready, 1)

            pool.wait_ge(v_by_act, 2 * B)
            pool.wait_ge(v_by_dve, 2 * B)
            load_values(0, 0)
            negate(0, 0)

            def units(b, tail, attn, last):
                for q in range(NQ):
                    u = NQ * b + q
                    if attn and not (last and q == NQ - 1):
                        hold(pool, pv_done, KT * u)
                        load_values(*following(b, q))
                    if q == 0 and tail:
                        pool.wait_ge(var_ready, b)
                        steps = Chain(pool, rstd2_step, b - 1)
                        steps.link(nc.gpsimd.tensor_scalar(rstd2[:, :], meanvar2[:, :, 1], EPS, None, ALU.add))
                        nc.gpsimd.tensor_tensor(rstd2[:, :], rstd2[:, :], minus_half[:, 0:QT],
                                                ALU.pow).then_inc(rstd2_ready, 1)
                    if attn and not (last and q == NQ - 1):
                        negate(*following(b, q))

            units(0, False, True, False)
            units(1, True, True, False)
            with pool.Fori(2, B - 1) as b:
                units(b, True, True, False)
            units(B - 1, True, True, True)
            units(B, True, False, True)

        @block.scalar
        def _(act):
            def first_part(i):
                b, c, bank, parts, cols = cuts[i]
                act.wait_ge(proj_ready, i + 1)
                if b is not None and b >= 2 and c == 0:
                    act.wait_ge(k_stored[b % 2], 16 * PARTS)
                nc.scalar.copy(parts[:, 0, cols], bank[:, 0:cols.stop - cols.start]).then_inc(hi_ready, 1)

            def second_part(i):
                _, _, _, parts, cols = cuts[i]
                act.wait_ge(rest_ready, i + 1)
                nc.scalar.copy(parts[:, 1, cols], rest[:, i % 2, 0:cols.stop - cols.start]).then_inc(mid_ready, 1)

            def cut_all(group):
                for i in group:
                    first_part(i)
                    if i > group[0]:
                        second_part(i - 1)
                second_part(group[-1])

            for b in range(B):
                cut_all(range(last_cut[b] - (CH - 1), last_cut[b] + 1))
                if b == 0:
                    for g in range(2):
                        act.wait_ge(xnT_ready, g + 1)
                        nc.scalar.copy(xnT[:, g * BANK:(g + 1) * BANK], (up_bank, down_bank)[g][:, :]).then_inc(xnT_copied, 1)
                    cut_all(range(last_q_cut - 1, last_q_cut + 1))
                    act.wait_ge(ld_w, 16 * 3)
                    nc.scalar.activation(gate_t[:, :], gates[:, :], ACT.Tanh).then_inc(gate_step, 1)
                for g in (0, 2):
                    act.wait_ge(v_ready, 4 * b + g + 1)
                    nc.scalar.copy(values[:, b, 4 * g:4 * g + 4, :],
                                   up_bank[:, :].rearrange("p (t n) -> p t n", n=D)).then_inc(v_by_act, 1)

            def exponentials(b, q, s):
                n = NQ * SLOTS * b + SLOTS * q + s
                act.wait_ge(scores_ready, n + 1)
                if s % QH == 0:
                    t, u = s // QH, NQ * b + q
                    if t == STEPS - 1:
                        hold(act, pv_done, KT * u)
                    elif t < 2:
                        hold(act, pv_done, KT * (u - 1) + 2 * (STEPS - 1 - 2 + t + 1))
                    else:
                        act.wait_ge(pv_done, KT * u + 2 * (t - 1))
                if s < QH * (STEPS - 1):
                    nc.scalar.activation(probs[:, s % (2 * QH), :], score_bank[s % 2][:, :], ACT.Exp,
                                         scale=SCALE).then_inc(probs_ready, 1)
                else:
                    nc.scalar.activation(probs_tail[0:TAIL, s % QH, :], score_bank[s % 2][0:TAIL, :], ACT.Exp,
                                         scale=SCALE).then_inc(probs_ready, 1)

            def neg_copy(b, q):
                act.wait_ge(neg_T, NQ * b + q + 1)
                hold(act, neg_in, 16 * PARTS * (NQ * b + q))
                nc.scalar.copy(neg_rows[:, :], down_b[0:PARTS * QH, 0:S]).then_inc(neg_rows_ready, 1)

            neg_copy(0, 0)

            def tanh_tile(b, n, bank):
                g = NT * (b - 1) + n
                act.wait_ge(up_ready, g + 1)
                hold(act, inner_ready, g - 1)
                nc.scalar.activation(th[:, n % 2, :], bank[:, 0:S], ACT.Tanh, scale=0.5).then_inc(th_ready, 1)

            def units(b, tail, attn, last):
                for q in range(NQ):
                    u = NQ * b + q
                    for s in range(SLOTS):
                        if attn:
                            exponentials(b, q, s)
                        if s == S_OCOPY and not (q == 0 and not tail) and (attn or q == 0):
                            act.wait_ge(pv_done, KT * u)
                            hold(act, out_T, u - 1)
                            nc.scalar.copy(head_outT[:, :], pv_bank[:, 0:S]).then_inc(out_copied, 1)
                        if s == S_MCOPY and attn and not (last and q == NQ - 1):
                            neg_copy(*following(b, q))
                        if tail and q == 0 and s == S_HTCOPY:
                            act.wait_ge(hT_ready, b)
                            nc.scalar.copy(headsT[:, :], up_bank[:, 0:S]).then_inc(hT_copied, 1)
                        if tail and q == 0 and s == S_XNCOPY:
                            act.wait_ge(xn2T_ready, b)
                            nc.scalar.copy(xn2T[:, :], up_bank[:, 0:S]).then_inc(xn2T_copied, 1)
                        if tail and q == 1 and s == 0:
                            act.wait_ge(rel_ready, b)
                            nc.scalar.activation(expo[:, :, :], rel[:, :, :], ACT.Exp).then_inc(expo_ready, 1)
                        for n in expert_work(q, s) if tail else ():
                            tanh_tile(b, n, up_bank if attn else up_banks[n % len(up_banks)])

            units(0, False, True, False)
            units(1, True, True, False)
            with act.Fori(2, B - 1) as b:
                units(b, True, True, False)
            units(B - 1, True, True, True)
            units(B, True, False, True)

        @block.vector
        def _(dve):
            dve.wait_ge(ld_x, 16)
            for i in range(B * QT):
                nc.vector.bn_stats(stats[:, i, :], xs[:, i, :]).then_inc(ln_step, 1)
            for i in range(B * QT):
                dve.wait_ge(ln_step, B * QT + i if i else B * QT)
                nc.vector.bn_aggr(meanvar[:, i, :], stats[:, i, :]).then_inc(ln_step, 1)
            dve.wait_ge(rstd_ready, 2)
            for i in range(B * QT):
                nc.vector.tensor_scalar(xn[:, i, :], xs[:, i, :], meanvar[:, i, 0:1], rstd[:, i:i + 1],
                                        ALU.subtract, ALU.mult).then_inc(xn_ready, 1)

            def masks(g):
                if g < QT:
                    dve.wait_ge(ld_mask, 16 * QT)
                else:
                    dve.wait_ge(ld_maskT, 16 * 3)
                if g < QT:
                    nc.vector.tensor_scalar(masked_q[:, g, :], mask_in[:, g, 0:SK], 0, None,
                                            ALU.is_equal).then_inc(mask_used, 1)
                    return
                n = 7 if g == QT else KT - 1 - 7
                src = mask_in[:, g - QT, 0:n * S].rearrange("p (t q) -> p t q", q=S)
                t0 = 7 * (g - QT)
                nc.vector.tensor_scalar(masked_k[:, t0:t0 + n, :], src, 0, None, ALU.is_equal).then_inc(mask_done, 1)
                if g == QT + 1:
                    nc.vector.tensor_scalar(masked_k[0:TAIL, KT - 1, :], mask_in[0:TAIL, 1, n * S:(n + 1) * S], 0, None,
                                            ALU.is_equal).then_inc(mask_done, 1)

            def cut_rest(i):
                _, _, bank, parts, cols = cuts[i]
                w = cols.stop - cols.start
                dve.wait_ge(hi_ready, i + 1)
                hold(dve, lo_ready, i - 1)
                nc.vector.tensor_tensor(rest[:, i % 2, 0:w], bank[:, 0:w], parts[:, 0, cols],
                                        ALU.subtract).then_inc(rest_ready, 1)

            def v_copy(b, g):
                if g == 1:
                    dve.wait_ge(v_ready, 4 * b + 2)
                    nc.vector.tensor_copy(values[:, b, 4:8, :],
                                          down_bank[:, :].rearrange("p (t n) -> p t n", n=D)).then_inc(v_by_dve, 1)
                if g == 3:
                    dve.wait_ge(v_ready, 4 * b + 4)
                    nc.vector.tensor_copy(values[0:TAIL, b, KT - 1, :], down_bank[0:TAIL, 0:D]).then_inc(v_by_dve, 1)

            for i in range(last_q_cut + 1):
                cut_rest(i)
            masks(0)
            masks(1)
            dve.wait_ge(mask_used, 2)
            nc.vector.reduce_max(row_masked[:, :], masked_q[:, :, :], axis=AX.XY).then_inc(mask_done, 1)
            v_copy(0, 1)
            v_copy(0, 3)
            for i in range(last_q_cut + 1, last_cut[1] + 1):
                cut_rest(i)
            v_copy(1, 1)
            v_copy(1, 3)
            dve.wait_ge(flag_sum, 1)
            nc.vector.tensor_copy(any_masked[:, :], down_bank[0:1, 0:1]).then_inc(flag_ready, 1)

            def chunk(b, q, n):
                dve.wait_ge(chunk_ready, NQ * CHUNKS * b + CHUNKS * q + n + 1)
                rows, bank = score_rows(n), max_bank[n % MAXB]
                if len(rows) == 1:
                    (row, c), = rows
                    dst, src = chunk_max[:, q % 2, row % QT, row // QT, c:c + 1], bank[:, 0:CW[c]]
                else:
                    j = rows[0][0] // QT
                    dst = chunk_max[:, q % 2, :, j:j + HALF // QT, CH - 1]
                    src = bank[:, 0:HALF * CW[-1]].rearrange("p (j t k) -> p t j k", t=QT, k=CW[-1])
                nc.vector.reduce_max(dst, src, axis=AX.X).then_inc(chunk_used, 1)
                if n == CHUNKS - 1:
                    u = NQ * b + q
                    dve.wait_ge(chunk_used, CHUNKS * (u + 1))
                    hold(dve, neg_parts_ready, u)
                    nc.vector.reduce_max(row_max[:, :, :], chunk_max[:, q % 2, :, :, :], axis=AX.X).then_inc(max_ready, 1)

            for m, (b, q, n) in enumerate(early):
                chunk(b, q, n)
                if m % 2 and 0 <= m // 2 - 1 < len(pieces):
                    kind, what = pieces[m // 2 - 1]
                    cut_rest(what) if kind == "K" else v_copy(*what)
                if m in (6, 14):
                    masks(2 if m == 6 else 3)
                if m == 18:
                    dve.wait_ge(gate_step, 1)
                    nc.vector.tensor_scalar(gate_t[:, 1:2], gate_t[:, 1:2], 0.5, None, ALU.mult).then_inc(gates_ready, 1)
                    dve.wait_ge(const_ready, 3)
                    nc.vector.tensor_copy(iota_f[:, :], iota_i[:, :]).then_inc(gates_ready, 1)

            def normalise(u, q):
                dve.wait_ge(out_T, u + 1)
                steps = Chain(dve, out_step, u)
                src = down_bank[:, 0:S].rearrange("p (t j c) -> p t j c", t=QT, j=QH)
                steps.link(nc.vector.reciprocal(denom[:, :, :], src[:, :, :, DH]))
                if q == 0:
                    hold(dve, hT_ready, u // NQ if isinstance(u, int) else batch_of[0])
                dst = heads[:, :, q * QH * DH:(q + 1) * QH * DH].rearrange("p t (j d) -> p t j d", d=DH)
                nc.vector.tensor_tensor(dst, src[:, :, :, 0:DH], denom[:, :, :, None].broadcast_to([P, QT, QH, DH]),
                                        ALU.mult).then_inc(heads_ready, 1)

            batch_of = [0]

            def residual(b):
                dve.wait_ge(attn_ready, b)
                dve.wait_ge(x_b_in, 16 * b)
                hold(dve, out_stored, 16 * (b - 1))
                steps = Chain(dve, tail_step, 2 * (b - 1))
                steps.link(nc.vector.scalar_tensor_tensor(
                    x1[:, :, :], down_bank[:, 0:S].rearrange("p (t n) -> p t n", n=D), gate_t[:, 0:1], x_b[:, :, :],
                    ALU.mult, ALU.add))
                for t in range(QT):
                    st = nc.vector.bn_stats(stats2[:, t, :], x1[:, t, :])
                steps.link(st)
                for t in range(QT):
                    mv = nc.vector.bn_aggr(meanvar2[:, t, :], stats2[:, t, :])
                mv.then_inc(var_ready, 1)

            def norm2(b):
                dve.wait_ge(rstd2_ready, b)
                for t in range(QT):
                    last = nc.vector.tensor_scalar(xn2[:, t, :], x1[:, t, :], meanvar2[:, t, 0:1], rstd2[:, t:t + 1],
                                                   ALU.subtract, ALU.mult)
                last.then_inc(xn2_ready, 1)

            def top2(b):
                dve.wait_ge(route_ready, b)
                steps = Chain(dve, route_step, 9 * (b - 1))
                steps.link(nc.vector.tensor_copy(logits[:, :, :], down_bank[:, 0:QT * E].rearrange("p (t e) -> p t e", e=E)))
                for t in range(QT):
                    m = nc.vector.max(top[:, t, :], logits[:, t, :])
                steps.link(m)
                for t in range(QT):
                    m = nc.vector.max_index(top_i[:, t, :], top[:, t, :], logits[:, t, :])
                steps.link(m)
                nc.vector.tensor_tensor(rel[:, :, :], logits[:, :, :], top[:, :, 0:1].broadcast_to([P, QT, E]),
                                        ALU.subtract).then_inc(rel_ready, 1)
                steps.link(nc.vector.tensor_copy(top_f[:, :, :], top_i[:, :, :]))

            def weights(b):
                steps = Chain(dve, route_step, 9 * (b - 1) + 4)
                iota = iota_f[:, None, :].broadcast_to([P, QT, E])
                nc.vector.tensor_tensor(first_hot[:, :, :], iota, top_f[:, :, 0:1].broadcast_to([P, QT, E]), ALU.is_equal)
                steps.link(nc.vector.tensor_tensor(second_hot[:, :, :], iota, top_f[:, :, 1:2].broadcast_to([P, QT, E]),
                                                   ALU.is_equal))
                dve.wait_ge(expo_ready, b)
                nc.vector.reduce_sum(total[:, :], expo[:, :, :], axis=AX.X)
                steps.link(nc.vector.tensor_tensor(first_hot[:, :, :], first_hot[:, :, :], second_hot[:, :, :], ALU.add))
                nc.vector.reciprocal(total[:, :], total[:, :])
                steps.link(nc.vector.tensor_tensor(first_hot[:, :, :], first_hot[:, :, :], expo[:, :, :], ALU.mult))
                steps.link(nc.vector.tensor_scalar(total[:, :], total[:, :], gate_t[:, 1:2], None, ALU.mult))
                steps.link(nc.vector.tensor_tensor(combine[:, :, :], first_hot[:, :, :],
                                                   total[:, :, None].broadcast_to([P, QT, E]), ALU.mult))

            def gate_tile(b, n, bank):
                g = NT * (b - 1) + n
                dve.wait_ge(th_ready, g + 1)
                hold(dve, inner_ready, g - 1)
                gated = (gated0, gated1)[n % 2]
                steps = Chain(dve, gated_step, g)
                steps.link(nc.vector.scalar_tensor_tensor(gated[:, :], th[:, n % 2, :], 1.0, bank[:, 0:S],
                                                          ALU.add, ALU.mult))
                hold(dve, down_ready, E * (b - 1) + n // TILES - 1)
                nc.vector.tensor_tensor(inner[:, n % 4, :], gated[:, :], bank[:, S:2 * S], ALU.mult).then_inc(inner_ready, 1)

            def add_expert(b, e, bank):
                g = E * (b - 1) + e
                dve.wait_ge(down_ready, g + 1)
                hold(dve, down_used, g)
                for t in range(QT):
                    last = nc.vector.scalar_tensor_tensor(x1[:, t, :], bank[:, t * D:(t + 1) * D],
                                                          combine[:, t, e:e + 1], x1[:, t, :], ALU.mult, ALU.add)
                last.then_inc(down_used, 1)

            def units(b, tail, attn, last):
                for q in range(NQ):
                    u = NQ * b + q
                    for s in range(SLOTS):
                        if attn:
                            by, n = divmod(s + LEAD, CHUNKS)
                            if not (last and q + 1 + by >= NQ):
                                chunk(*following(b, q, 1 + by), n)
                        if s == S_ONORM and not (q == 0 and not tail) and (attn or q == 0):
                            batch_of[0] = b
                            normalise(u - 1, (q - 1) % NQ)
                        if tail and q == 0:
                            if s == S_X1:
                                residual(b)
                            if s == S_XN:
                                norm2(b)
                            if s == S_TOP:
                                top2(b)
                        if tail and attn and q == 1 and s == 1:
                            weights(b)
                        for n in expert_work(q, s, 1) if tail and attn else ():
                            gate_tile(b, n, up_bank)
                        for n in expert_work(q, s, DOWN_AFTER + 1) if tail and attn else ():
                            if n % TILES == TILES - 1:
                                add_expert(b, n // TILES, down_bank)

            units(0, False, True, False)
            units(1, True, True, False)
            with dve.Fori(2, B - 1) as b:
                units(b, True, True, False)
            units(B - 1, True, True, True)
            units(B, True, False, True)
            for n in range(NT):
                gate_tile(B, n, up_banks[n % len(up_banks)])
                if n == 1:
                    weights(B)
                if n % TILES == 0 and n >= 2 * TILES:
                    add_expert(B, n // TILES - 2, down_banks[(n // TILES - 2) % len(down_banks)])
            for e in (E - 2, E - 1):
                add_expert(B, e, down_banks[e % len(down_banks)])

        @block.tensor
        def _(pe):
            def project(i):
                b, c, bank, _, cols = cuts[i]
                if b is None:
                    pe.wait_ge(xnT_copied, c + 1)
                    w, src = wq, xnT[:, cols]
                else:
                    if c == 0:
                        pe.wait_ge(ld_ctx[b % 2], 16 * (b // 2 + 1))
                    w, src = wk, ctx_in[:, b % 2, cols]
                hold(pe, rest_ready, i - 2)
                nc.tensor.matmul(bank[:, 0:cols.stop - cols.start], w[:, :], src, start=True, stop=True).then_inc(proj_ready, 1)

            def project_values(b, g):
                if b == 0 and g < 2:
                    pe.wait_ge(xnT_copied, g + 1)
                else:
                    pe.wait_ge(v_by_dve if g % 2 else v_by_act, 2 * b + g // 2)
                for t in range(4 * g, min(4 * g + 4, KT)):
                    w = P if t < KT - 1 else TAIL
                    v = nc.tensor.matmul((up_bank, down_bank)[g % 2][0:w, (t % 4) * D:(t % 4 + 1) * D],
                                         ctx_in[:, b % 2, t * P:t * P + w], wv[:, :], start=True, stop=True)
                v.then_inc(v_ready, 1)

            pe.wait_ge(ld_wk, 16)
            for c in range(CH):
                project(c)
            pe.wait_ge(ident_ready, 3)
            for i in range(B * QT):
                pe.wait_ge(xn_ready, i + 1)
                bank = (up_bank, down_bank)[i // 4]
                last = nc.tensor.transpose(bank[:, (i % 4) * P:(i % 4 + 1) * P], xn[:, i, :], ident[:, :])
                if i % 4 == 3:
                    last.then_inc(xnT_ready, 1)
            pe.wait_ge(ld_w, 16 * 3)
            for c in range(2):
                project(last_q_cut - 1 + c)
            pe.wait_ge(ld_wv, 16)
            for g in range(4):
                project_values(0, g)
            for c in range(CH):
                project(last_q_cut + 1 + c)
            for g in range(4):
                project_values(1, g)
            pe.wait_ge(mask_done, 1)
            pe.wait_ge(const_ready, 1)
            pe.wait_ge(v_by_dve, 4)
            nc.tensor.matmul(down_bank[0:1, 0:1], row_masked[:, :], ones_col[:, :],
                             start=True, stop=True).then_inc(flag_sum, 1)
            pe.wait_ge(flag_ready, 1)
            masked = pe.value_load(any_masked[0:1, 0:1], min_val=0, max_val=P)

            def attention(with_mask):

                def chunk(b, q, n):
                    if n == 0:
                        pe.wait_ge(ld_unit[q], 16 * (PARTS + 1) * (b + 1))
                    hold(pe, chunk_used, NQ * CHUNKS * b + CHUNKS * q + n + 1 - bank_free(n))
                    for i, (row, c) in enumerate(score_rows(n)):
                        j, t = row // QT, row % QT
                        dst = max_bank[n % MAXB][:, i * CW[c]:(i + 1) * CW[c]]
                        last = nc.tensor.matmul(dst, queries[q][0:ROWS, j, t * P:(t + 1) * P],
                                                keys[q][0:ROWS, j, c * BANK:c * BANK + CW[c]], start=True, stop=not with_mask)
                        if with_mask:
                            last = nc.tensor.matmul(dst, ident_neg[:, :], masked_q[:, t, c * BANK:c * BANK + CW[c]],
                                                    start=False, stop=True)
                    last.then_inc(chunk_ready, 1)

                def scores(b, q, s):
                    if s == 0:
                        pe.wait_ge(neg_in, 16 * PARTS * (NQ * b + q + 1))
                    hold(pe, probs_ready, NQ * SLOTS * b + SLOTS * q + s - 1)
                    for i in range(2):
                        j, t = (s % QH, 2 * (s // QH) + i) if s < QH * (STEPS - 1) else (2 * (s % QH) + i, KT - 1)
                        w = P if t < KT - 1 else TAIL
                        dst = score_bank[s % 2][0:w, i * S:(i + 1) * S]
                        last = nc.tensor.matmul(dst, keys[q][0:KR, j, t * P:t * P + w], queries[q][0:KR, j, :],
                                                start=True, stop=not with_mask)
                        if with_mask:
                            last = nc.tensor.matmul(dst, ident_neg[0:w, 0:w], masked_k[0:w, t, :], start=False, stop=True)
                    last.then_inc(scores_ready, 1)

                def probs_v(u, q, kt):
                    pe.wait_ge(probs_ready, SLOTS * u + min(QH * (kt // 2 + 1), SLOTS))
                    if kt == 0:
                        pe.wait_ge(values_ready, 2 * (u + 1))
                        hold(pe, out_copied, u)
                    w = P if kt < KT - 1 else TAIL
                    for j in range(QH):
                        if kt < KT - 1:
                            p = probs[:, QH * (kt // 2 % 2) + j, (kt % 2) * S:(kt % 2 + 1) * S]
                        else:
                            p = probs_tail[0:w, j // 2, (j % 2) * S:(j % 2 + 1) * S]
                        last = nc.tensor.matmul(pv_bank[VW * j:VW * (j + 1), 0:S], value_t[q % 2][0:w, kt, j, :], p,
                                                start=kt == 0, stop=kt == KT - 1)
                    last.then_inc(pv_done, 1)

                def neg_transpose(b, q):
                    u = NQ * b + q
                    pe.wait_ge(neg_parts_ready, u + 1)
                    for t in range(QT):
                        last = nc.tensor.transpose(down_b[0:PARTS * QH, t * P:(t + 1) * P],
                                                   neg_parts[:, t, :, :].rearrange("p c j -> p (c j)"), ident_b[:, :])
                    last.then_inc(neg_T, 1)

                def down_bank_free(b, tail, q, s, attn, last):
                    u = NQ * b + q
                    hold(pe, heads_ready, (u if s > S_OTR else u - 1) if attn or q == 0 else NQ * b)
                    if attn:
                        pe.wait_ge(neg_rows_ready, u + 2 if s > S_MTR and not (last and q == NQ - 1) else u + 1)
                    if tail:
                        hold(pe, down_used, E * (b - 1) + experts_done(q, s))
                        if q == 0 and s > S_ROUTE or q > 0:
                            pe.wait_ge(rel_ready, b)
                        elif q == 0 and s > S_PROJ:
                            pe.wait_ge(var_ready, b)

                def expert_up(b, n, banks):
                    e, i = n // TILES, n % TILES
                    hold(pe, inner_ready, NT * (b - 1) + n + 1 - len(banks))
                    if n == 0:
                        pe.wait_ge(xn2T_copied, b)
                    for k in range(2):
                        last = nc.tensor.matmul(banks[n % len(banks)][:, k * S:(k + 1) * S], w1[:, e, k * INTER + i * P:k * INTER + (i + 1) * P],
                                                xn2T[:, :], start=True, stop=True)
                    last.then_inc(up_ready, 1)

                def expert_down(b, e, bank):
                    pe.wait_ge(inner_ready, NT * (b - 1) + TILES * (e + 1))
                    for t in range(QT):
                        for i in range(TILES):
                            last = nc.tensor.matmul(bank[:, t * D:(t + 1) * D],
                                                    inner[:, (TILES * e + i) % 4, t * P:(t + 1) * P], w2[:, e, i, :],
                                                    start=i == 0, stop=i == TILES - 1)
                    last.then_inc(down_ready, 1)

                def tail_slot(b, s):
                    if s == S_HT:
                        pe.wait_ge(ld_fw, 16 * 4)
                        pe.wait_ge(heads_ready, NQ * b)
                        hold(pe, inner_ready, NT * (b - 1))
                        for t in range(QT):
                            last = nc.tensor.transpose(up_bank[:, t * P:(t + 1) * P], heads[:, t, :], ident[:, :])
                        last.then_inc(hT_ready, 1)
                    if s == S_PROJ:
                        pe.wait_ge(hT_copied, b)
                        for t in range(QT):
                            last = nc.tensor.matmul(down_bank[:, t * D:(t + 1) * D], headsT[:, t * P:(t + 1) * P], wt[:, :],
                                                    start=True, stop=True)
                        last.then_inc(attn_ready, 1)
                    if s == S_XNTR:
                        pe.wait_ge(xn2_ready, b)
                        for t in range(QT):
                            last = nc.tensor.transpose(up_bank[:, t * P:(t + 1) * P], xn2[:, t, :], ident[:, :])
                        last.then_inc(xn2T_ready, 1)
                    if s == S_ROUTE:
                        pe.wait_ge(xn2T_copied, b)
                        for t in range(QT):
                            last = nc.tensor.matmul(down_bank[:, t * E:(t + 1) * E], xn2T[:, t * P:(t + 1) * P], wr[:, :],
                                                    start=True, stop=True)
                        last.then_inc(route_ready, 1)

                def units(b, tail, attn, last):
                    for q in range(NQ):
                        u = NQ * b + q
                        for s in range(SLOTS):
                            before = not (q == 0 and not tail) and (attn or q == 0)
                            if attn:
                                scores(b, q, s)
                                by, n = divmod(s + LEAD, CHUNKS)
                                if not (last and q + 1 + by >= NQ):
                                    chunk(*following(b, q, 1 + by), n)
                            for back, kt in value_tiles(s):
                                if before if back else attn:
                                    probs_v(u - back, (q - back) % NQ, kt)
                            if s == S_OTR and before:
                                pe.wait_ge(out_copied, u)
                                down_bank_free(b, tail, q, s, attn, last)
                                for t in range(QT):
                                    tr = nc.tensor.transpose(down_bank[:, t * P:(t + 1) * P],
                                                             head_outT[:, t * P:(t + 1) * P], ident[:, :])
                                tr.then_inc(out_T, 1)
                            if s == S_MTR and attn and not (last and q == NQ - 1):
                                down_bank_free(b, tail, q, s, attn, last)
                                neg_transpose(*following(b, q))
                            if tail and q == 0:
                                if s in (S_PROJ, S_ROUTE):
                                    down_bank_free(b, tail, q, s, attn, last)
                                tail_slot(b, s)
                            for n in expert_work(q, s) if tail and attn else ():
                                expert_up(b, n, [up_bank])
                            for n in expert_work(q, s, DOWN_AFTER) if tail and attn else ():
                                if n % TILES == TILES - 1:
                                    down_bank_free(b, tail, q, s, attn, last)
                                    expert_down(b, n // TILES, down_bank)

                for m, (b, q, n) in enumerate(early):
                    chunk(b, q, n)
                    if m % 2 and m // 2 < len(pieces):
                        kind, what = pieces[m // 2]
                        project(what) if kind == "K" else project_values(*what)
                pe.wait_ge(v_by_act, 2 * B)
                pe.wait_ge(v_by_dve, 2 * B)
                pe.wait_ge(rest_ready, len(cuts))
                neg_transpose(0, 0)
                if with_mask:
                    pe.wait_ge(mask_done, 4)
                units(0, False, True, False)
                units(1, True, True, False)
                with pe.Fori(2, B - 1) as b:
                    units(b, True, True, False)
                units(B - 1, True, True, True)
                units(B, True, False, True)

                def last_down(e):
                    pe.wait_ge(down_used, E * (B - 1) + max(0, e + 1 - len(down_banks)))
                    if e == 0:
                        pe.wait_ge(rel_ready, B)
                    expert_down(B, e, down_banks[e % len(down_banks)])

                for n in range(NT):
                    expert_up(B, n, up_banks)
                    if n % TILES == TILES - 1 and n > TILES:
                        last_down(n // TILES - 1)
                last_down(E - 1)

            with pe.If(masked != 0):
                attention(True)
            with pe.Else():
                attention(False)


def kernel(**inputs):
    import concourse.bacc as bacc
    from concourse.bass_utils import run_bass_kernel_spmd

    a = {k: np.asarray(v) for k, v in inputs.items()}
    mask = a["mask_1x1xSxS2_if1"][0, 0]
    arrays = {
        "x": a["x"],
        "ctxT": a["ctx_1024"].transpose(0, 2, 1),
        "mask": mask,
        "maskT": mask.T,
        "g_x": a["g_xattn"],
        "g_f": a["g_ffn"],
        "W_Q": a["L0_xattn_W_Q"],
        "W_K": a["L0_xattn_W_K"],
        "W_V": a["L0_xattn_W_V"],
        "W_T": a["L0_xattn_W_T"],
        "w1T": a["L0_ffn_w1"].reshape(E * 2 * INTER, D).T,
        "w2T": a["L0_ffn_w2"].transpose(0, 2, 1),
        "rT": a["L0_ffn_router_w"].T,
    }
    arrays = {k: np.ascontiguousarray(v) for k, v in arrays.items()}
    nc = bacc.Bacc("TRN2", target_bir_lowering=False, num_devices=1)
    args = [nc.dram_tensor(k, v.shape, mybir.dt.from_np(v.dtype), kind="ExternalInput").ap() for k, v in arrays.items()]
    out = nc.dram_tensor("out", (B, S, D), FP32, kind="ExternalOutput").ap()
    block_kernel(nc, *args, out)
    r = run_bass_kernel_spmd(nc, [arrays], core_ids=[0])
    return r.results[0]["out"]
```

```python
from contextlib import ExitStack

import numpy as np

import concourse.bass as bass
from concourse import mybir

FP32, BF16 = mybir.dt.float32, mybir.dt.bfloat16
I32, U32 = mybir.dt.int32, mybir.dt.uint32
ALU, ACT, AX = mybir.AluOpType, mybir.ActivationFunctionType, mybir.AxisListType

P = 128
B, S, D = 4, 256, 128
SK = 1601
H, DH = 16, 8
E, INTER = 8, 256
QH = 4
NQ = H // QH
QT = S // P
KT = -(-SK // P)
TAIL = SK - (KT - 1) * P
PARTS = 3
ROWS = PARTS * PARTS * DH
NEG = ROWS
KR = ROWS + PARTS
BANK = 512
CH = -(-SK // BANK)
CW = [min(BANK, SK - c * BANK) for c in range(CH)]
HALF = QH * QT // 2
MAXB = 3
CHUNKS = 2 * (HALF * (CH - 1) + 1)
STEPS = (KT + 1) // 2
SLOTS = QH * (STEPS - 1) + QH // 2
LEAD = 10
TILES = INTER // P
NT = E * TILES
CTX = 2
VW = 32
EPS = 1e-5
MASKED = -float(2 ** 100)
SCALE = 1.0 / float(np.sqrt(DH))

S_OCOPY, S_OTR, S_ONORM = 3, 8, 8
S_MTR, S_MCOPY = 19, 19
S_HT, S_HTCOPY, S_PROJ, S_X1, S_XN, S_XNTR, S_XNCOPY, S_ROUTE, S_TOP = 12, 13, 14, 14, 18, 20, 20, 22, 22
TILE_AT = [4 + n * ((NQ - 1) * SLOTS - 9) // NT for n in range(NT)]
MASK_AT = (3, 4)
NEG_AT = 4
DOWN_AFTER = 6
assert not {(at + DOWN_AFTER) % SLOTS for at in TILE_AT[TILES - 1::TILES]} & {S_OTR, S_MTR}


def hold(eng, sem, n):
    if not isinstance(n, int) or n > 0:
        eng.wait_ge(sem, n)


class Chain:

    def __init__(self, eng, sem, start=0):
        self.eng, self.sem, self.n = eng, sem, start

    def link(self, ins):
        ins.then_inc(self.sem, 1)
        self.n = self.n + 1
        self.eng.wait_ge(self.sem, self.n)


def following(b, q, by=1):
    return (b + (q + by) // NQ, (q + by) % NQ)


def score_rows(n):
    half, i = divmod(n, CHUNKS // 2)
    if i < HALF * (CH - 1):
        return [(half * HALF + i // (CH - 1), i % (CH - 1))]
    return [(half * HALF + r, CH - 1) for r in range(HALF)]


def bank_free(n):
    return MAXB if n >= MAXB else next(CHUNKS + n - m for m in reversed(range(CHUNKS)) if m % MAXB == n)


def expert_work(q, s, after=0):
    return [n for n in range(NT) if TILE_AT[n] + after == (q - 1) * SLOTS + s]


def experts_done(q, s):
    return sum(TILE_AT[TILES * e + TILES - 1] + DOWN_AFTER < (q - 1) * SLOTS + s for e in range(E))


def value_tiles(s):
    at = [QH * (t // 2) + QH + 1 + 2 * (t % 2) for t in range(KT - 1)] + [SLOTS + 2]
    return [(at[t] // SLOTS, t) for t in range(KT) if at[t] % SLOTS == s]


def block_kernel(nc, x, ctxT, mask, maskT, g_x, g_f, W_Q, W_K, W_V, W_T, w1T, w2T, rT, out):
    es = ExitStack()
    sb = lambda name, shape, dt: es.enter_context(nc.sbuf_tensor(name, shape, dt))
    ps = lambda name, dt=FP32: es.enter_context(nc.psum_tensor(name, [P, BANK * 4 // (2 if dt == BF16 else 4)], dt))
    sem = lambda name: es.enter_context(nc.semaphore(name))

    with es:
        k_parts_dram = nc.dram_tensor("k_parts", [B, H, PARTS, DH, SK], BF16).ap()
        q_parts_dram = nc.dram_tensor("q_parts", [H, PARTS, PARTS, DH, B * S], BF16).ap()

        wq, wk, wv, wt = (sb(n, [P, D], FP32) for n in ("wq", "wk", "wv", "wt"))
        w2 = sb("w2", [P, E, TILES, D], FP32)
        wr = sb("wr", [P, E], FP32)
        gates = sb("gates", [P, 2], FP32)
        gate_t = sb("gate_t", [P, 2], FP32)
        ctx_in = sb("ctx_in", [P, CTX, SK], FP32)
        masked_q = sb("masked_q", [P, QT, SK], BF16)
        masked_k = sb("masked_k", [P, KT, S], BF16)
        ones_row = sb("ones_row", [PARTS, SK], BF16)
        most_masked = sb("most_masked", [1, 1], FP32)
        any_masked = sb("any_masked", [1, 1], I32)
        ident = sb("ident", [P, P], FP32)
        ident_b = sb("ident_b", [P, P], BF16)
        ident_neg = sb("ident_neg", [P, P], BF16)
        ones_col = sb("ones_col", [P, 1], BF16)
        iota_i = sb("iota_i", [P, E], I32)
        iota_f = sb("iota_f", [P, E], FP32)
        minus_half = sb("minus_half", [P, B * QT], FP32)
        xs = sb("xs", [P, B * QT, D], FP32)
        stats = sb("stats", [P, B * QT, 6], FP32)
        meanvar = sb("meanvar", [P, B * QT, 2], FP32)
        rstd = sb("rstd", [P, B * QT], FP32)
        split0 = sb("split0", [P, PARTS, SK], BF16)
        rest = sb("rest", [P, 2, BANK], FP32)
        keys = [sb(f"keys{i}", [P, QH, SK], BF16) for i in range(NQ)]
        queries = [sb(f"queries{i}", [P, QH, S], BF16) for i in range(NQ)]
        values = sb("values", [P, B, KT, D], FP32)
        value_t = [sb(f"value_t{i}", [P, KT, QH, VW], FP32) for i in range(2)]
        probs = sb("probs", [P, 2 * QH, 2 * S], FP32)
        probs_tail = sb("probs_tail", [P, QH // 2, 2 * S], FP32)
        chunk_max = sb("chunk_max", [P, 2, QT, QH, CH], FP32)
        row_max = sb("row_max", [P, QT, QH], FP32)
        neg_max = sb("neg_max", [P, QT, QH], FP32)
        neg_rest = sb("neg_rest", [P, QT, QH], FP32)
        neg_parts = sb("neg_parts", [P, QT, PARTS, QH], BF16)
        neg_rows = sb("neg_rows", [PARTS * QH, S], BF16)
        head_outT = sb("head_outT", [P, S], FP32)
        denom = sb("denom", [P, QT, QH], FP32)
        heads = sb("heads", [P, QT, D], FP32)
        x1 = sb("x1", [P, QT, D], FP32)
        stats2 = sb("stats2", [P, QT, 6], FP32)
        meanvar2 = sb("meanvar2", [P, QT, 2], FP32)
        rstd2 = sb("rstd2", [P, QT], FP32)
        logits = sb("logits", [P, QT, E], FP32)
        top = sb("top", [P, QT, 8], FP32)
        top_i = sb("top_i", [P, QT, 8], U32)
        top_f = sb("top_f", [P, QT, 8], FP32)
        rel = sb("rel", [P, QT, E], FP32)
        expo = sb("expo", [P, QT, E], FP32)
        first_hot = sb("first_hot", [P, QT, E], FP32)
        second_hot = sb("second_hot", [P, QT, E], FP32)
        total = sb("total", [P, QT], FP32)
        combine = sb("combine", [P, QT, E], FP32)
        w1 = sb("w1", [P, E, 2 * INTER], FP32)
        late = sb("late", [P, 12 * S], FP32)
        headsT, xn2T, gated0, gated1 = (late[:, i * S:(i + 1) * S] for i in (0, 1, 2, 11))
        x_b, xn2 = (late[:, i * S:(i + 1) * S].rearrange("p (t d) -> p t d", d=D) for i in (3, 4))
        th = late[:, 5 * S:7 * S].rearrange("p (n s) -> p n s", s=S)
        inner = late[:, 7 * S:11 * S].rearrange("p (n s) -> p n s", s=S)
        mask_in = w1[:, :, :].rearrange("p e i -> p (e i)").bitcast(I32).rearrange("p (g k) -> p g k", g=2)
        spare = probs[:, :, :].rearrange("p a b -> p (a b)")
        xn = spare[:, 0:B * S].rearrange("p (t d) -> p t d", d=D)
        xnT = spare[:, B * S:2 * B * S]
        q_split = spare[:, 2 * B * S:4 * B * S].bitcast(BF16)[:, 0:PARTS * B * S].rearrange("p (c t) -> p c t", c=PARTS)
        split1 = late[:, :].bitcast(BF16)[:, 0:PARTS * SK].rearrange("p (c k) -> p c k", c=PARTS)
        splits = [split0, split1]

        max_bank = [ps(f"max_bank{i}") for i in range(MAXB)]
        score_bank = [ps("score_bank0"), ps("score_bank1")]
        pv_bank = ps("pv_bank")
        up_bank = ps("up_bank")
        down_bank = ps("down_bank")
        down_b = down_bank[:, :].bitcast(BF16)
        cuts = [(0, c) for c in range(CH)] + [(None, c) for c in range(2)] + [(b, c) for b in range(1, B) for c in range(CH)]
        cut_banks = score_bank + [pv_bank]
        cuts = [(b, c, cut_banks[i % 3], q_split if b is None else splits[b % 2],
                 slice(c * BANK, c * BANK + (BANK if b is None else CW[c]))) for i, (b, c) in enumerate(cuts)]
        last_cut = [max(i for i, x in enumerate(cuts) if x[0] == b) for b in range(B)]
        last_q_cut = max(i for i, x in enumerate(cuts) if x[0] is None)
        pieces = [("V", (1, g)) for g in range(4)] + [("K", i) for i in range(last_cut[1] + 1, len(cuts))]
        late_pieces = [(b, g) for b in range(2, B) for g in range(4)]
        assert len(pieces) < CHUNKS // 2 and NEG_AT < len(late_pieces) <= LEAD
        up_banks, down_banks = [up_bank] + score_bank, [down_bank] + max_bank
        value_banks = [max_bank[0], max_bank[1], max_bank[2], max_bank[1]]

        ld_x, ld_wk, ld_wv, ld_w, ld_fw, ld_mask = (
            sem("ld_x"), sem("ld_wk"), sem("ld_wv"), sem("ld_w"), sem("ld_fw"), sem("ld_mask"))
        ld_ctx = [sem(f"ld_ctx{b}") for b in range(B)]
        const_ready, ident_ready = sem("const_ready"), sem("ident_ready")
        zeroed = sem("zeroed")
        rows_ready = sem("rows_ready")
        ln_step, rstd_ready, xn_ready = sem("ln_step"), sem("rstd_ready"), sem("xn_ready")
        xnT_ready, xnT_copied = sem("xnT_ready"), sem("xnT_copied")
        proj_ready, hi_ready, rest_ready, mid_ready, lo_ready = (
            sem("proj_ready"), sem("hi_ready"), sem("rest_ready"), sem("mid_ready"), sem("lo_ready"))
        v_ready, v_by_act, v_by_dve = sem("v_ready"), sem("v_by_act"), sem("v_by_dve")
        q_stored, k_stored, ones_rows = sem("q_stored"), [sem(f"k_stored{i}") for i in range(2)], sem("ones_rows")
        q_rest_stored, ld_maskT = sem("q_rest_stored"), sem("ld_maskT")
        mask_used, mask_done, flag_sum, flag_ready = (
            sem("mask_used"), sem("mask_done"), sem("flag_sum"), sem("flag_ready"))
        flag_step = sem("flag_step")
        gate_step, gates_ready = sem("gate_step"), sem("gates_ready")
        ld_unit = [sem(f"ld_unit{i}") for i in range(NQ)]
        chunk_ready, chunk_used = sem("chunk_ready"), sem("chunk_used")
        max_ready, neg_step, neg_parts_ready = sem("max_ready"), sem("neg_step"), sem("neg_parts_ready")
        neg_T, neg_rows_ready, neg_in = sem("neg_T"), sem("neg_rows_ready"), sem("neg_in")
        scores_ready, probs_ready, pv_done = sem("scores_ready"), sem("probs_ready"), sem("pv_done")
        values_ready = sem("values_ready")
        out_copied, out_T, out_step, heads_ready = sem("out_copied"), sem("out_T"), sem("out_step"), sem("heads_ready")
        hT_ready, hT_copied, attn_ready = sem("hT_ready"), sem("hT_copied"), sem("attn_ready")
        x_b_in, tail_step, var_ready, rstd2_ready, xn2_ready = (
            sem("x_b_in"), sem("tail_step"), sem("var_ready"), sem("rstd2_ready"), sem("xn2_ready"))
        rstd2_step = sem("rstd2_step")
        xn2T_ready, xn2T_copied, route_ready = sem("xn2T_ready"), sem("xn2T_copied"), sem("route_ready")
        rel_ready, expo_ready, route_step = sem("rel_ready"), sem("expo_ready"), sem("route_step")
        up_ready, th_ready, gated_step, inner_ready = sem("up_ready"), sem("th_ready"), sem("gated_step"), sem("inner_ready")
        down_ready, down_used, out_stored = sem("down_ready"), sem("down_used"), sem("out_stored")

        block = es.enter_context(nc.Block())

        @block.sync
        def _(sp):
            x_rows = x.rearrange("b (t p) d -> p (b t) d", p=P)
            out_rows = out.rearrange("b (t p) d -> b p t d", p=P)

            def load_ctx(b):
                if b >= CTX:
                    sp.wait_ge(v_ready, 4 * (b - CTX + 1))
                sp.dma_start(ctx_in[:, b % CTX, :], ctxT[b]).then_inc(ld_ctx[b], 16)

            def load_unit(b, q):
                h0 = QH * q
                for c in range(PARTS):
                    rows = slice(c * PARTS * DH, (c + 1) * PARTS * DH)
                    sp.dma_start(keys[q][rows, :, :],
                                 k_parts_dram[b, h0:h0 + QH].rearrange("j p d k -> (p d) j k")).then_inc(ld_unit[q], 16)
                sp.dma_start(queries[q][0:ROWS, :, :],
                             q_parts_dram[h0:h0 + QH, :, :, :, bass.ds(b * S, S)].rearrange("j c p d t -> (c p d) j t")
                             ).then_inc(ld_unit[q], 16)

            def load_neg(b, q):
                sp.wait_ge(neg_rows_ready, NQ * b + q + 1)
                for p in range(PARTS):
                    sp.dma_start(queries[q][NEG + p:NEG + p + 1, :, :], neg_rows[p * QH:(p + 1) * QH, :]).then_inc(neg_in, 16)

            def store_keys(b):
                sp.wait_ge(lo_ready, last_cut[b] + 1)
                for p in range(PARTS):
                    sp.dma_start(k_parts_dram[b, :, p], splits[b % 2][:, p, :]).then_inc(k_stored[b % 2], 16)

            sp.dma_start(xs[:, :, :], x_rows).then_inc(ld_x, 16)
            sp.dma_start(wk[:, :], W_K).then_inc(ld_wk, 16)
            load_ctx(0)
            sp.dma_start(wq[:, :], W_Q).then_inc(ld_w, 16)
            sp.dma_start(gates[:, 0:1], g_x.rearrange("(o g) -> o g", o=1).broadcast_to([P, 1])).then_inc(ld_w, 16)
            sp.dma_start(gates[:, 1:2], g_f.rearrange("(o g) -> o g", o=1).broadcast_to([P, 1])).then_inc(ld_w, 16)
            sp.dma_start(wv[:, :], W_V).then_inc(ld_wv, 16)
            for t in range(QT):
                sp.dma_start(mask_in[:, t, 0:SK], mask.rearrange("(t p) k -> p t k", p=P)[:, t, :]).then_inc(ld_mask, 16)
            load_ctx(1)
            store_keys(0)
            def store_queries(tokens, stored):
                for c in range(PARTS):
                    for p in range(PARTS):
                        sp.dma_start(q_parts_dram[:, c, p, :, tokens], q_split[:, c, tokens]).then_inc(stored, 16)

            sp.wait_ge(lo_ready, last_q_cut)
            store_queries(slice(0, S), q_stored)
            sp.wait_ge(k_stored[0], 16 * PARTS)
            sp.wait_ge(q_stored, 16 * PARTS * PARTS)
            load_unit(0, 0)
            load_unit(0, 1)
            load_ctx(2)
            sp.wait_ge(rows_ready, 1)
            for i in range(NQ):
                sp.dma_start(keys[i][NEG:KR, :, :], ones_row[:, None, :].broadcast_to([PARTS, QH, SK])
                             ).then_inc(ones_rows, 16)
            store_keys(1)
            load_ctx(3)
            sp.wait_ge(lo_ready, last_q_cut + 1)
            store_queries(slice(S, B * S), q_rest_stored)
            store_keys(2)
            store_keys(3)
            sp.wait_ge(q_rest_stored, 16 * PARTS * PARTS)
            sp.wait_ge(k_stored[0], 16 * PARTS * 2)
            sp.wait_ge(k_stored[1], 16 * PARTS * 2)
            sp.wait_ge(ones_rows, 16 * NQ)
            load_neg(0, 0)
            sp.wait_ge(mask_done, 3)
            sp.dma_start(w1[:, :, :], w1T.rearrange("d (e i) -> d e i", e=E)).then_inc(ld_fw, 16)
            sp.dma_start(w2[:, :, :, :], w2T.rearrange("e (t p) h -> p e t h", p=P)).then_inc(ld_fw, 16)
            sp.dma_start(wt[:, :], W_T).then_inc(ld_fw, 16)
            sp.dma_start(wr[:, :], rT).then_inc(ld_fw, 16)

            def units(b, tail, attn, last):
                for q in range(NQ):
                    u = NQ * b + q
                    if q == 0 and tail:
                        if not isinstance(b, int) or b >= 2:
                            sp.wait_ge(down_used, E * (b - 1))
                            sp.dma_start(out_rows[b - 2], x1[:, :, :]).then_inc(out_stored, 16)
                        hold(sp, var_ready, b - 1)
                        sp.dma_start(x_b[:, :, :], x[b - 1].rearrange("(t p) d -> p t d", p=P)).then_inc(x_b_in, 16)
                    if not attn:
                        continue
                    if not (last and q >= NQ - 2):
                        hold(sp, scores_ready, SLOTS * (u - 1))
                        load_unit(*following(b, q, 2))
                    if not (last and q == NQ - 1):
                        load_neg(*following(b, q))

            units(0, False, True, False)
            units(1, True, True, False)
            with sp.Fori(2, B - 1) as b:
                units(b, True, True, False)
            units(B - 1, True, True, True)
            units(B, True, False, True)
            sp.wait_ge(down_used, E * B)
            sp.dma_start(out_rows[B - 1], x1[:, :, :]).then_inc(out_stored, 16)
            sp.wait_ge(out_stored, 16 * B)

        @block.gpsimd
        def _(pool):
            nc.gpsimd.memset(minus_half[:, :], -0.5).then_inc(const_ready, 1)
            nc.gpsimd.memset(ident[:, :], 0.0).then_inc(zeroed, 1)
            nc.gpsimd.memset(ident_b[:, :], 0.0).then_inc(zeroed, 1)
            nc.gpsimd.memset(ident_neg[:, :], 0.0).then_inc(zeroed, 1)
            pool.wait_ge(zeroed, 3)
            for m, fill in ((ident, 1.0), (ident_b, 1.0), (ident_neg, MASKED)):
                nc.gpsimd.affine_select(out=m[:, :], in_=m[:, :], compare_op=ALU.not_equal, fill=fill, base=0,
                                        pattern=[[-1, P]], channel_multiplier=1).then_inc(ident_ready, 1)
            def third_part(i):
                _, _, _, parts, cols = cuts[i]
                pool.wait_ge(mid_ready, i + 1)
                nc.gpsimd.tensor_tensor(parts[:, 2, cols], rest[:, i % 2, 0:cols.stop - cols.start], parts[:, 1, cols],
                                        ALU.subtract).then_inc(lo_ready, 1)

            def load_values(b, q):
                i, cols = q % 2, slice(q * QH * DH, (q + 1) * QH * DH)
                nc.gpsimd.tensor_copy(value_t[i][:, 0:KT - 1, :, 0:DH],
                                      values[:, b, 0:KT - 1, cols].rearrange("p t (j d) -> p t j d", d=DH)
                                      ).then_inc(values_ready, 1)
                nc.gpsimd.tensor_copy(value_t[i][0:TAIL, KT - 1, :, 0:DH],
                                      values[0:TAIL, b, KT - 1, cols].rearrange("p (j d) -> p j d", d=DH)
                                      ).then_inc(values_ready, 1)

            pool.wait_ge(ln_step, 2 * B * QT)
            pool.wait_ge(const_ready, 1)
            chain = Chain(pool, rstd_ready)
            chain.link(nc.gpsimd.tensor_scalar(rstd[:, :], meanvar[:, :, 1], EPS, None, ALU.add))
            nc.gpsimd.tensor_tensor(rstd[:, :], rstd[:, :], minus_half[:, :], ALU.pow).then_inc(rstd_ready, 1)
            nc.gpsimd.memset(ones_col[:, :], 1.0).then_inc(const_ready, 1)
            nc.gpsimd.iota(iota_i[:, :], pattern=[[1, E]], base=0, channel_multiplier=0).then_inc(const_ready, 1)
            for i in range(len(cuts)):
                third_part(i)
                if i == CH - 1:
                    nc.gpsimd.memset(ones_row[:, :], 1.0).then_inc(rows_ready, 1)
                if i == last_q_cut:
                    for i in range(2):
                        nc.gpsimd.memset(value_t[i][:, :, :, :], 0.0).then_inc(const_ready, 1)
                    pool.wait_ge(const_ready, 5)
                    for i in range(2):
                        nc.gpsimd.memset(value_t[i][:, :, :, DH:DH + 1], 1.0).then_inc(const_ready, 1)
                if i == last_cut[1]:
                    for g in range(2):
                        pool.wait_ge(mask_used, g + 1)
                        n = 7 if g == 0 else KT - 1 - 7
                        pool.dma_start(mask_in[:, g, 0:n * S].rearrange("p (t q) -> p t q", q=S),
                                       maskT[g * 7 * P:(g * 7 + n) * P, :].rearrange("(t p) q -> p t q", p=P)
                                       ).then_inc(ld_maskT, 16)
                    pool.dma_start(mask_in[0:TAIL, 1, (KT - 8) * S:(KT - 7) * S], maskT[(KT - 1) * P:SK, :]).then_inc(ld_maskT, 16)
                    pool.wait_ge(v_by_act, 2)
                    pool.wait_ge(v_by_dve, 2)
                    pool.wait_ge(const_ready, 7)
                    load_values(0, 0)

            def negate(b, q):
                u = NQ * b + q
                pool.wait_ge(max_ready, u + 1)
                hold(pool, neg_T, u)
                steps = Chain(pool, neg_step, 4 * u)
                part = [neg_parts[:, :, p, :] for p in range(PARTS)]
                steps.link(nc.gpsimd.tensor_scalar(neg_max[:, :, :], row_max[:, :, :], -1.0, None, ALU.mult))
                steps.link(nc.gpsimd.tensor_copy(part[0], neg_max[:, :, :]))
                steps.link(nc.gpsimd.tensor_tensor(neg_rest[:, :, :], neg_max[:, :, :], part[0], ALU.subtract))
                steps.link(nc.gpsimd.tensor_copy(part[1], neg_rest[:, :, :]))
                nc.gpsimd.tensor_tensor(part[2], neg_rest[:, :, :], part[1], ALU.subtract).then_inc(neg_parts_ready, 1)

            negate(0, 0)
            pool.wait_ge(v_by_act, 2 * B)
            pool.wait_ge(v_by_dve, 2 * B)

            def units(b, tail, attn, last):
                for q in range(NQ):
                    u = NQ * b + q
                    if attn and not (last and q == NQ - 1):
                        hold(pool, pv_done, KT * u)
                        load_values(*following(b, q))
                    if q == 0 and tail:
                        pool.wait_ge(var_ready, b)
                        steps = Chain(pool, rstd2_step, b - 1)
                        steps.link(nc.gpsimd.tensor_scalar(rstd2[:, :], meanvar2[:, :, 1], EPS, None, ALU.add))
                        nc.gpsimd.tensor_tensor(rstd2[:, :], rstd2[:, :], minus_half[:, 0:QT],
                                                ALU.pow).then_inc(rstd2_ready, 1)
                    if attn and not (last and q == NQ - 1):
                        negate(*following(b, q))

            units(0, False, True, False)
            units(1, True, True, False)
            with pool.Fori(2, B - 1) as b:
                units(b, True, True, False)
            units(B - 1, True, True, True)
            units(B, True, False, True)

        @block.scalar
        def _(act):
            def first_part(i):
                b, c, bank, parts, cols = cuts[i]
                act.wait_ge(proj_ready, i + 1)
                if b is not None and b >= 2 and c == 0:
                    act.wait_ge(k_stored[b % 2], 16 * PARTS)
                nc.scalar.copy(parts[:, 0, cols], bank[:, 0:cols.stop - cols.start]).then_inc(hi_ready, 1)

            def second_part(i):
                _, _, _, parts, cols = cuts[i]
                act.wait_ge(rest_ready, i + 1)
                nc.scalar.copy(parts[:, 1, cols], rest[:, i % 2, 0:cols.stop - cols.start]).then_inc(mid_ready, 1)

            def cut_all(group):
                for i in group:
                    first_part(i)
                    if i > group[0]:
                        second_part(i - 1)
                second_part(group[-1])

            def v_copy(b, g, bank):
                act.wait_ge(v_ready, 4 * b + g + 1)
                nc.scalar.copy(values[:, b, 4 * g:4 * g + 4, :],
                               bank[:, :].rearrange("p (t n) -> p t n", n=D)).then_inc(v_by_act, 1)

            def xnT_copy(g):
                act.wait_ge(xnT_ready, g + 1)
                nc.scalar.copy(xnT[:, g * BANK:(g + 1) * BANK], (up_bank, down_bank)[g][:, :]).then_inc(xnT_copied, 1)

            for i in range(CH - 1):
                first_part(i)
            for g in range(2):
                xnT_copy(g)
                second_part(g)
            first_part(CH - 1)
            second_part(CH - 2)
            first_part(CH)
            second_part(CH - 1)
            second_part(CH)
            v_copy(0, 0, value_banks[0])
            first_part(CH + 1)
            second_part(CH + 1)
            v_copy(0, 2, value_banks[2])
            act.wait_ge(ld_w, 16 * 3)
            nc.scalar.activation(gate_t[:, :], gates[:, :], ACT.Tanh).then_inc(gate_step, 1)
            cut_all(range(last_q_cut + 1, last_cut[1] + 1))
            v_copy(1, 0, up_bank)
            v_copy(1, 2, up_bank)
            cut_all(range(last_cut[1] + 1, last_cut[2] + 1))
            cut_all(range(last_cut[2] + 1, last_cut[3] + 1))

            def exponentials(b, q, s):
                n = NQ * SLOTS * b + SLOTS * q + s
                act.wait_ge(scores_ready, n + 1)
                if s % QH == 0:
                    t, u = s // QH, NQ * b + q
                    if t == STEPS - 1:
                        hold(act, pv_done, KT * u)
                    elif t < 2:
                        hold(act, pv_done, KT * (u - 1) + 2 * (STEPS - 1 - 2 + t + 1))
                    else:
                        act.wait_ge(pv_done, KT * u + 2 * (t - 1))
                if s < QH * (STEPS - 1):
                    nc.scalar.activation(probs[:, s % (2 * QH), :], score_bank[s % 2][:, :], ACT.Exp,
                                         scale=SCALE).then_inc(probs_ready, 1)
                else:
                    nc.scalar.activation(probs_tail[0:TAIL, s % QH, :], score_bank[s % 2][0:TAIL, :], ACT.Exp,
                                         scale=SCALE).then_inc(probs_ready, 1)

            def neg_copy(b, q):
                act.wait_ge(neg_T, NQ * b + q + 1)
                hold(act, neg_in, 16 * PARTS * (NQ * b + q))
                nc.scalar.copy(neg_rows[:, :], down_b[0:PARTS * QH, 0:S]).then_inc(neg_rows_ready, 1)

            for m, (b, g) in enumerate(late_pieces):
                if m == NEG_AT:
                    neg_copy(0, 0)
                if g % 2 == 0:
                    v_copy(b, g, up_bank)

            def tanh_tile(b, n, bank):
                g = NT * (b - 1) + n
                act.wait_ge(up_ready, g + 1)
                hold(act, inner_ready, g - 1)
                nc.scalar.activation(th[:, n % 2, :], bank[:, 0:S], ACT.Tanh, scale=0.5).then_inc(th_ready, 1)

            def units(b, tail, attn, last):
                for q in range(NQ):
                    u = NQ * b + q
                    for s in range(SLOTS):
                        if attn:
                            exponentials(b, q, s)
                        if s == S_OCOPY and not (q == 0 and not tail) and (attn or q == 0):
                            act.wait_ge(pv_done, KT * u)
                            hold(act, out_T, u - 1)
                            nc.scalar.copy(head_outT[:, :], pv_bank[:, 0:S]).then_inc(out_copied, 1)
                        if s == S_MCOPY and attn and not (last and q == NQ - 1):
                            neg_copy(*following(b, q))
                        if tail and q == 0 and s == S_HTCOPY:
                            act.wait_ge(hT_ready, b)
                            nc.scalar.copy(headsT[:, :], up_bank[:, 0:S]).then_inc(hT_copied, 1)
                        if tail and q == 0 and s == S_XNCOPY:
                            act.wait_ge(xn2T_ready, b)
                            nc.scalar.copy(xn2T[:, :], up_bank[:, 0:S]).then_inc(xn2T_copied, 1)
                        if tail and q == 1 and s == 0:
                            act.wait_ge(rel_ready, b)
                            nc.scalar.activation(expo[:, :, :], rel[:, :, :], ACT.Exp).then_inc(expo_ready, 1)
                        for n in expert_work(q, s) if tail else ():
                            tanh_tile(b, n, up_bank if attn else up_banks[n % len(up_banks)])

            units(0, False, True, False)
            units(1, True, True, False)
            with act.Fori(2, B - 1) as b:
                units(b, True, True, False)
            units(B - 1, True, True, True)
            units(B, True, False, True)

        @block.vector
        def _(dve):
            dve.wait_ge(ld_x, 16)
            for i in range(B * QT):
                nc.vector.bn_stats(stats[:, i, :], xs[:, i, :]).then_inc(ln_step, 1)
            for i in range(B * QT):
                dve.wait_ge(ln_step, B * QT + i if i else B * QT)
                nc.vector.bn_aggr(meanvar[:, i, :], stats[:, i, :]).then_inc(ln_step, 1)
            dve.wait_ge(rstd_ready, 2)
            for i in range(B * QT):
                nc.vector.tensor_scalar(xn[:, i, :], xs[:, i, :], meanvar[:, i, 0:1], rstd[:, i:i + 1],
                                        ALU.subtract, ALU.mult).then_inc(xn_ready, 1)

            def masks(g):
                if g < QT:
                    dve.wait_ge(ld_mask, 16 * QT)
                else:
                    dve.wait_ge(ld_maskT, 16 * 3)
                if g < QT:
                    nc.vector.tensor_scalar(masked_q[:, g, :], mask_in[:, g, 0:SK], 0, None,
                                            ALU.is_equal).then_inc(mask_used, 1)
                    return
                n = 7 if g == QT else KT - 1 - 7
                src = mask_in[:, g - QT, 0:n * S].rearrange("p (t q) -> p t q", q=S)
                t0 = 7 * (g - QT)
                nc.vector.tensor_scalar(masked_k[:, t0:t0 + n, :], src, 0, None, ALU.is_equal).then_inc(mask_done, 1)
                if g == QT + 1:
                    nc.vector.tensor_scalar(masked_k[0:TAIL, KT - 1, :], mask_in[0:TAIL, 1, n * S:(n + 1) * S], 0, None,
                                            ALU.is_equal).then_inc(mask_done, 1)

            def cut_rest(i):
                _, _, bank, parts, cols = cuts[i]
                w = cols.stop - cols.start
                dve.wait_ge(hi_ready, i + 1)
                hold(dve, lo_ready, i - 1)
                nc.vector.tensor_tensor(rest[:, i % 2, 0:w], bank[:, 0:w], parts[:, 0, cols],
                                        ALU.subtract).then_inc(rest_ready, 1)

            def v_copy(b, g):
                bank = value_banks[g] if b == 0 else down_bank
                if g == 1:
                    dve.wait_ge(v_ready, 4 * b + 2)
                    nc.vector.tensor_copy(values[:, b, 4:8, :],
                                          bank[:, :].rearrange("p (t n) -> p t n", n=D)).then_inc(v_by_dve, 1)
                if g == 3:
                    dve.wait_ge(v_ready, 4 * b + 4)
                    nc.vector.tensor_copy(values[0:TAIL, b, KT - 1, :], bank[0:TAIL, 0:D]).then_inc(v_by_dve, 1)

            for i in range(CH):
                cut_rest(i)
            cut_rest(CH)
            v_copy(0, 1)
            cut_rest(CH + 1)
            v_copy(0, 3)
            masks(0)
            masks(1)
            for i in range(last_q_cut + 1, last_cut[1] + 1):
                cut_rest(i)
            dve.wait_ge(flag_sum, 1)
            nc.vector.reduce_max(most_masked[:, :], down_bank[0:1, :], axis=AX.X).then_inc(flag_step, 1)
            dve.wait_ge(flag_step, 1)
            nc.vector.tensor_copy(any_masked[:, :], most_masked[:, :]).then_inc(flag_ready, 1)

            def chunk(b, q, n):
                dve.wait_ge(chunk_ready, NQ * CHUNKS * b + CHUNKS * q + n + 1)
                rows, bank = score_rows(n), max_bank[n % MAXB]
                if len(rows) == 1:
                    (row, c), = rows
                    dst, src = chunk_max[:, q % 2, row % QT, row // QT, c:c + 1], bank[:, 0:CW[c]]
                else:
                    j = rows[0][0] // QT
                    dst = chunk_max[:, q % 2, :, j:j + HALF // QT, CH - 1]
                    src = bank[:, 0:HALF * CW[-1]].rearrange("p (j t k) -> p t j k", t=QT, k=CW[-1])
                nc.vector.reduce_max(dst, src, axis=AX.X).then_inc(chunk_used, 1)
                if n == CHUNKS - 1:
                    u = NQ * b + q
                    dve.wait_ge(chunk_used, CHUNKS * (u + 1))
                    hold(dve, neg_parts_ready, u)
                    nc.vector.reduce_max(row_max[:, :, :], chunk_max[:, q % 2, :, :, :], axis=AX.X).then_inc(max_ready, 1)

            for n in range(CHUNKS):
                chunk(0, 0, n)
                if n % 2 and 0 <= n // 2 - 1 < len(pieces):
                    kind, what = pieces[n // 2 - 1]
                    cut_rest(what) if kind == "K" else v_copy(*what)
            for n in range(LEAD):
                chunk(0, 1, n)
                if n < len(late_pieces):
                    v_copy(*late_pieces[n])
                if n in MASK_AT:
                    masks(QT + MASK_AT.index(n))
            dve.wait_ge(gate_step, 1)
            nc.vector.tensor_scalar(gate_t[:, 1:2], gate_t[:, 1:2], 0.5, None, ALU.mult).then_inc(gates_ready, 1)
            dve.wait_ge(const_ready, 3)
            nc.vector.tensor_copy(iota_f[:, :], iota_i[:, :]).then_inc(gates_ready, 1)

            def normalise(u, q):
                dve.wait_ge(out_T, u + 1)
                steps = Chain(dve, out_step, u)
                src = down_bank[:, 0:S].rearrange("p (t j c) -> p t j c", t=QT, j=QH)
                steps.link(nc.vector.reciprocal(denom[:, :, :], src[:, :, :, DH]))
                if q == 0:
                    hold(dve, hT_ready, u // NQ if isinstance(u, int) else batch_of[0])
                dst = heads[:, :, q * QH * DH:(q + 1) * QH * DH].rearrange("p t (j d) -> p t j d", d=DH)
                nc.vector.tensor_tensor(dst, src[:, :, :, 0:DH], denom[:, :, :, None].broadcast_to([P, QT, QH, DH]),
                                        ALU.mult).then_inc(heads_ready, 1)

            batch_of = [0]

            def residual(b):
                dve.wait_ge(attn_ready, b)
                dve.wait_ge(x_b_in, 16 * b)
                hold(dve, out_stored, 16 * (b - 1))
                steps = Chain(dve, tail_step, 2 * (b - 1))
                steps.link(nc.vector.scalar_tensor_tensor(
                    x1[:, :, :], down_bank[:, 0:S].rearrange("p (t n) -> p t n", n=D), gate_t[:, 0:1], x_b[:, :, :],
                    ALU.mult, ALU.add))
                for t in range(QT):
                    st = nc.vector.bn_stats(stats2[:, t, :], x1[:, t, :])
                steps.link(st)
                for t in range(QT):
                    mv = nc.vector.bn_aggr(meanvar2[:, t, :], stats2[:, t, :])
                mv.then_inc(var_ready, 1)

            def norm2(b):
                dve.wait_ge(rstd2_ready, b)
                for t in range(QT):
                    last = nc.vector.tensor_scalar(xn2[:, t, :], x1[:, t, :], meanvar2[:, t, 0:1], rstd2[:, t:t + 1],
                                                   ALU.subtract, ALU.mult)
                last.then_inc(xn2_ready, 1)

            def top2(b):
                dve.wait_ge(route_ready, b)
                steps = Chain(dve, route_step, 9 * (b - 1))
                steps.link(nc.vector.tensor_copy(logits[:, :, :], down_bank[:, 0:QT * E].rearrange("p (t e) -> p t e", e=E)))
                for t in range(QT):
                    m = nc.vector.max(top[:, t, :], logits[:, t, :])
                steps.link(m)
                for t in range(QT):
                    m = nc.vector.max_index(top_i[:, t, :], top[:, t, :], logits[:, t, :])
                steps.link(m)
                nc.vector.tensor_tensor(rel[:, :, :], logits[:, :, :], top[:, :, 0:1].broadcast_to([P, QT, E]),
                                        ALU.subtract).then_inc(rel_ready, 1)
                steps.link(nc.vector.tensor_copy(top_f[:, :, :], top_i[:, :, :]))

            def weights(b):
                steps = Chain(dve, route_step, 9 * (b - 1) + 4)
                iota = iota_f[:, None, :].broadcast_to([P, QT, E])
                nc.vector.tensor_tensor(first_hot[:, :, :], iota, top_f[:, :, 0:1].broadcast_to([P, QT, E]), ALU.is_equal)
                steps.link(nc.vector.tensor_tensor(second_hot[:, :, :], iota, top_f[:, :, 1:2].broadcast_to([P, QT, E]),
                                                   ALU.is_equal))
                dve.wait_ge(expo_ready, b)
                nc.vector.reduce_sum(total[:, :], expo[:, :, :], axis=AX.X)
                steps.link(nc.vector.tensor_tensor(first_hot[:, :, :], first_hot[:, :, :], second_hot[:, :, :], ALU.add))
                nc.vector.reciprocal(total[:, :], total[:, :])
                steps.link(nc.vector.tensor_tensor(first_hot[:, :, :], first_hot[:, :, :], expo[:, :, :], ALU.mult))
                steps.link(nc.vector.tensor_scalar(total[:, :], total[:, :], gate_t[:, 1:2], None, ALU.mult))
                steps.link(nc.vector.tensor_tensor(combine[:, :, :], first_hot[:, :, :],
                                                   total[:, :, None].broadcast_to([P, QT, E]), ALU.mult))

            def gate_tile(b, n, bank):
                g = NT * (b - 1) + n
                dve.wait_ge(th_ready, g + 1)
                hold(dve, inner_ready, g - 1)
                gated = (gated0, gated1)[n % 2]
                steps = Chain(dve, gated_step, g)
                steps.link(nc.vector.scalar_tensor_tensor(gated[:, :], th[:, n % 2, :], 1.0, bank[:, 0:S],
                                                          ALU.add, ALU.mult))
                hold(dve, down_ready, E * (b - 1) + n // TILES - 1)
                nc.vector.tensor_tensor(inner[:, n % 4, :], gated[:, :], bank[:, S:2 * S], ALU.mult).then_inc(inner_ready, 1)

            def add_expert(b, e, bank):
                g = E * (b - 1) + e
                dve.wait_ge(down_ready, g + 1)
                hold(dve, down_used, g)
                for t in range(QT):
                    last = nc.vector.scalar_tensor_tensor(x1[:, t, :], bank[:, t * D:(t + 1) * D],
                                                          combine[:, t, e:e + 1], x1[:, t, :], ALU.mult, ALU.add)
                last.then_inc(down_used, 1)

            def units(b, tail, attn, last):
                for q in range(NQ):
                    u = NQ * b + q
                    for s in range(SLOTS):
                        if attn:
                            by, n = divmod(s + LEAD, CHUNKS)
                            if not (last and q + 1 + by >= NQ):
                                chunk(*following(b, q, 1 + by), n)
                        if s == S_ONORM and not (q == 0 and not tail) and (attn or q == 0):
                            batch_of[0] = b
                            normalise(u - 1, (q - 1) % NQ)
                        if tail and q == 0:
                            if s == S_X1:
                                residual(b)
                            if s == S_XN:
                                norm2(b)
                            if s == S_TOP:
                                top2(b)
                        if tail and attn and q == 1 and s == 1:
                            weights(b)
                        for n in expert_work(q, s) if tail and attn else ():
                            gate_tile(b, n, up_bank)
                        for n in expert_work(q, s, DOWN_AFTER) if tail and attn else ():
                            if n % TILES == TILES - 1:
                                add_expert(b, n // TILES, down_bank)

            units(0, False, True, False)
            units(1, True, True, False)
            with dve.Fori(2, B - 1) as b:
                units(b, True, True, False)
            units(B - 1, True, True, True)
            units(B, True, False, True)
            for n in range(NT):
                gate_tile(B, n, up_banks[n % len(up_banks)])
                if n == 1:
                    weights(B)
                if n % TILES == 0 and n >= 2 * TILES:
                    add_expert(B, n // TILES - 2, down_banks[(n // TILES - 2) % len(down_banks)])
            for e in (E - 2, E - 1):
                add_expert(B, e, down_banks[e % len(down_banks)])

        @block.tensor
        def _(pe):
            def project(i):
                b, c, bank, _, cols = cuts[i]
                if b is None:
                    pe.wait_ge(xnT_copied, c + 1)
                    w, src = wq, xnT[:, cols]
                else:
                    if c == 0:
                        pe.wait_ge(ld_ctx[b], 16)
                    w, src = wk, ctx_in[:, b % CTX, cols]
                hold(pe, rest_ready, i - 2)
                nc.tensor.matmul(bank[:, 0:cols.stop - cols.start], w[:, :], src, start=True, stop=True).then_inc(proj_ready, 1)

            def project_values(b, g):
                if b == 0:
                    hold(pe, v_by_dve, g // 2 if g % 2 else 0)
                    bank = value_banks[g]
                else:
                    pe.wait_ge(v_by_dve if g % 2 else v_by_act, 2 * b + g // 2)
                    bank = (up_bank, down_bank)[g % 2]
                for t in range(4 * g, min(4 * g + 4, KT)):
                    w = P if t < KT - 1 else TAIL
                    v = nc.tensor.matmul(bank[0:w, (t % 4) * D:(t % 4 + 1) * D],
                                         ctx_in[:, b % CTX, t * P:t * P + w], wv[:, :], start=True, stop=True)
                v.then_inc(v_ready, 1)

            pe.wait_ge(ld_wk, 16)
            for c in range(CH - 1):
                project(c)
            pe.wait_ge(ident_ready, 3)
            for i in range(B * QT):
                pe.wait_ge(xn_ready, i + 1)
                bank = (up_bank, down_bank)[i // 4]
                last = nc.tensor.transpose(bank[:, (i % 4) * P:(i % 4 + 1) * P], xn[:, i, :], ident[:, :])
                if i % 4 == 3:
                    last.then_inc(xnT_ready, 1)
            project(CH - 1)
            pe.wait_ge(ld_w, 16 * 3)
            project(CH)
            pe.wait_ge(ld_wv, 16)
            project_values(0, 0)
            project_values(0, 1)
            project(CH + 1)
            project_values(0, 2)
            project_values(0, 3)
            pe.wait_ge(mask_used, QT)
            pe.wait_ge(const_ready, 2)
            for t in range(QT):
                for c in range(CH):
                    count = nc.tensor.matmul(down_bank[0:1, 0:CW[c]], ones_col[:, :],
                                             masked_q[:, t, c * BANK:c * BANK + CW[c]],
                                             start=t == 0 and c == 0, stop=t == QT - 1 and c == CH - 1)
            count.then_inc(flag_sum, 1)
            for c in range(CH):
                project(last_q_cut + 1 + c)
            pe.wait_ge(flag_ready, 1)
            masked = pe.value_load(any_masked[0:1, 0:1], min_val=0, max_val=QT * CH * P)

            def attention(with_mask):

                def chunk(b, q, n):
                    if n == 0:
                        pe.wait_ge(ld_unit[q], 16 * (PARTS + 1) * (b + 1))
                    hold(pe, chunk_used, NQ * CHUNKS * b + CHUNKS * q + n + 1 - bank_free(n))
                    for i, (row, c) in enumerate(score_rows(n)):
                        j, t = row // QT, row % QT
                        dst = max_bank[n % MAXB][:, i * CW[c]:(i + 1) * CW[c]]
                        last = nc.tensor.matmul(dst, queries[q][0:ROWS, j, t * P:(t + 1) * P],
                                                keys[q][0:ROWS, j, c * BANK:c * BANK + CW[c]], start=True, stop=not with_mask)
                        if with_mask:
                            last = nc.tensor.matmul(dst, ident_neg[:, :], masked_q[:, t, c * BANK:c * BANK + CW[c]],
                                                    start=False, stop=True)
                    last.then_inc(chunk_ready, 1)

                def scores(b, q, s):
                    if s == 0:
                        pe.wait_ge(neg_in, 16 * PARTS * (NQ * b + q + 1))
                    hold(pe, probs_ready, NQ * SLOTS * b + SLOTS * q + s - 1)
                    for i in range(2):
                        j, t = (s % QH, 2 * (s // QH) + i) if s < QH * (STEPS - 1) else (2 * (s % QH) + i, KT - 1)
                        w = P if t < KT - 1 else TAIL
                        dst = score_bank[s % 2][0:w, i * S:(i + 1) * S]
                        last = nc.tensor.matmul(dst, keys[q][0:KR, j, t * P:t * P + w], queries[q][0:KR, j, :],
                                                start=True, stop=not with_mask)
                        if with_mask:
                            last = nc.tensor.matmul(dst, ident_neg[0:w, 0:w], masked_k[0:w, t, :], start=False, stop=True)
                    last.then_inc(scores_ready, 1)

                def probs_v(u, q, kt):
                    pe.wait_ge(probs_ready, SLOTS * u + min(QH * (kt // 2 + 1), SLOTS))
                    if kt == 0:
                        pe.wait_ge(values_ready, 2 * (u + 1))
                        hold(pe, out_copied, u)
                    w = P if kt < KT - 1 else TAIL
                    for j in range(QH):
                        if kt < KT - 1:
                            p = probs[:, QH * (kt // 2 % 2) + j, (kt % 2) * S:(kt % 2 + 1) * S]
                        else:
                            p = probs_tail[0:w, j // 2, (j % 2) * S:(j % 2 + 1) * S]
                        last = nc.tensor.matmul(pv_bank[VW * j:VW * (j + 1), 0:S], value_t[q % 2][0:w, kt, j, :], p,
                                                start=kt == 0, stop=kt == KT - 1)
                    last.then_inc(pv_done, 1)

                def neg_transpose(b, q):
                    u = NQ * b + q
                    pe.wait_ge(neg_parts_ready, u + 1)
                    for t in range(QT):
                        last = nc.tensor.transpose(down_b[0:PARTS * QH, t * P:(t + 1) * P],
                                                   neg_parts[:, t, :, :].rearrange("p c j -> p (c j)"), ident_b[:, :])
                    last.then_inc(neg_T, 1)

                def down_bank_free(b, tail, q, s, attn, last):
                    u = NQ * b + q
                    hold(pe, heads_ready, (u if s > S_OTR else u - 1) if attn or q == 0 else NQ * b)
                    if attn:
                        pe.wait_ge(neg_rows_ready, u + 2 if s > S_MTR and not (last and q == NQ - 1) else u + 1)
                    if tail:
                        hold(pe, down_used, E * (b - 1) + experts_done(q, s))
                        if q == 0 and s > S_ROUTE or q > 0:
                            pe.wait_ge(rel_ready, b)
                        elif q == 0 and s > S_PROJ:
                            pe.wait_ge(var_ready, b)

                def expert_up(b, n, banks):
                    e, i = n // TILES, n % TILES
                    hold(pe, inner_ready, NT * (b - 1) + n + 1 - len(banks))
                    if n == 0:
                        pe.wait_ge(xn2T_copied, b)
                    for k in range(2):
                        last = nc.tensor.matmul(banks[n % len(banks)][:, k * S:(k + 1) * S], w1[:, e, k * INTER + i * P:k * INTER + (i + 1) * P],
                                                xn2T[:, :], start=True, stop=True)
                    last.then_inc(up_ready, 1)

                def expert_down(b, e, bank):
                    pe.wait_ge(inner_ready, NT * (b - 1) + TILES * (e + 1))
                    for t in range(QT):
                        for i in range(TILES):
                            last = nc.tensor.matmul(bank[:, t * D:(t + 1) * D],
                                                    inner[:, (TILES * e + i) % 4, t * P:(t + 1) * P], w2[:, e, i, :],
                                                    start=i == 0, stop=i == TILES - 1)
                    last.then_inc(down_ready, 1)

                def tail_slot(b, s):
                    if s == S_HT:
                        pe.wait_ge(ld_fw, 16 * 4)
                        pe.wait_ge(heads_ready, NQ * b)
                        hold(pe, inner_ready, NT * (b - 1))
                        for t in range(QT):
                            last = nc.tensor.transpose(up_bank[:, t * P:(t + 1) * P], heads[:, t, :], ident[:, :])
                        last.then_inc(hT_ready, 1)
                    if s == S_PROJ:
                        pe.wait_ge(hT_copied, b)
                        for t in range(QT):
                            last = nc.tensor.matmul(down_bank[:, t * D:(t + 1) * D], headsT[:, t * P:(t + 1) * P], wt[:, :],
                                                    start=True, stop=True)
                        last.then_inc(attn_ready, 1)
                    if s == S_XNTR:
                        pe.wait_ge(xn2_ready, b)
                        for t in range(QT):
                            last = nc.tensor.transpose(up_bank[:, t * P:(t + 1) * P], xn2[:, t, :], ident[:, :])
                        last.then_inc(xn2T_ready, 1)
                    if s == S_ROUTE:
                        pe.wait_ge(xn2T_copied, b)
                        for t in range(QT):
                            last = nc.tensor.matmul(down_bank[:, t * E:(t + 1) * E], xn2T[:, t * P:(t + 1) * P], wr[:, :],
                                                    start=True, stop=True)
                        last.then_inc(route_ready, 1)

                def units(b, tail, attn, last):
                    for q in range(NQ):
                        u = NQ * b + q
                        for s in range(SLOTS):
                            before = not (q == 0 and not tail) and (attn or q == 0)
                            if attn:
                                scores(b, q, s)
                                by, n = divmod(s + LEAD, CHUNKS)
                                if not (last and q + 1 + by >= NQ):
                                    chunk(*following(b, q, 1 + by), n)
                            for back, kt in value_tiles(s):
                                if before if back else attn:
                                    probs_v(u - back, (q - back) % NQ, kt)
                            if s == S_OTR and before:
                                pe.wait_ge(out_copied, u)
                                down_bank_free(b, tail, q, s, attn, last)
                                for t in range(QT):
                                    tr = nc.tensor.transpose(down_bank[:, t * P:(t + 1) * P],
                                                             head_outT[:, t * P:(t + 1) * P], ident[:, :])
                                tr.then_inc(out_T, 1)
                            if s == S_MTR and attn and not (last and q == NQ - 1):
                                down_bank_free(b, tail, q, s, attn, last)
                                neg_transpose(*following(b, q))
                            if tail and q == 0:
                                if s in (S_PROJ, S_ROUTE):
                                    down_bank_free(b, tail, q, s, attn, last)
                                tail_slot(b, s)
                            for n in expert_work(q, s) if tail and attn else ():
                                expert_up(b, n, [up_bank])
                            for n in expert_work(q, s, DOWN_AFTER) if tail and attn else ():
                                if n % TILES == TILES - 1:
                                    down_bank_free(b, tail, q, s, attn, last)
                                    expert_down(b, n // TILES, down_bank)

                pe.wait_ge(v_by_act, 2)
                pe.wait_ge(v_by_dve, 2)
                for n in range(CHUNKS):
                    chunk(0, 0, n)
                    if n % 2 and n // 2 < len(pieces):
                        kind, what = pieces[n // 2]
                        project(what) if kind == "K" else project_values(*what)
                for n in range(LEAD):
                    if n == NEG_AT:
                        pe.wait_ge(v_by_dve, 2 * 2 + sum(g % 2 for _, g in late_pieces[:NEG_AT]))
                        neg_transpose(0, 0)
                    chunk(0, 1, n)
                    if n < len(late_pieces):
                        b, g = late_pieces[n]
                        if g % 2 and n >= NEG_AT:
                            pe.wait_ge(neg_rows_ready, 1)
                        project_values(b, g)
                pe.wait_ge(v_by_act, 2 * B)
                pe.wait_ge(v_by_dve, 2 * B)
                pe.wait_ge(rest_ready, len(cuts))
                if with_mask:
                    pe.wait_ge(mask_done, 3)
                units(0, False, True, False)
                units(1, True, True, False)
                with pe.Fori(2, B - 1) as b:
                    units(b, True, True, False)
                units(B - 1, True, True, True)
                units(B, True, False, True)

                def last_down(e):
                    pe.wait_ge(down_used, E * (B - 1) + max(0, e + 1 - len(down_banks)))
                    if e == 0:
                        pe.wait_ge(rel_ready, B)
                    expert_down(B, e, down_banks[e % len(down_banks)])

                for n in range(NT):
                    expert_up(B, n, up_banks)
                    if n % TILES == TILES - 1 and n > TILES:
                        last_down(n // TILES - 1)
                last_down(E - 1)

            with pe.If(masked != 0):
                attention(True)
            with pe.Else():
                attention(False)


def kernel(**inputs):
    import concourse.bacc as bacc
    from concourse.bass_utils import run_bass_kernel_spmd

    a = {k: np.asarray(v) for k, v in inputs.items()}
    mask = a["mask_1x1xSxS2_if1"][0, 0]
    arrays = {
        "x": a["x"],
        "ctxT": a["ctx_1024"].transpose(0, 2, 1),
        "mask": mask,
        "maskT": mask.T,
        "g_x": a["g_xattn"],
        "g_f": a["g_ffn"],
        "W_Q": a["L0_xattn_W_Q"],
        "W_K": a["L0_xattn_W_K"],
        "W_V": a["L0_xattn_W_V"],
        "W_T": a["L0_xattn_W_T"],
        "w1T": a["L0_ffn_w1"].reshape(E * 2 * INTER, D).T,
        "w2T": a["L0_ffn_w2"].transpose(0, 2, 1),
        "rT": a["L0_ffn_router_w"].T,
    }
    arrays = {k: np.ascontiguousarray(v) for k, v in arrays.items()}
    nc = bacc.Bacc("TRN2", target_bir_lowering=False, num_devices=1)
    args = [nc.dram_tensor(k, v.shape, mybir.dt.from_np(v.dtype), kind="ExternalInput").ap() for k, v in arrays.items()]
    out = nc.dram_tensor("out", (B, S, D), FP32, kind="ExternalOutput").ap()
    block_kernel(nc, *args, out)
    r = run_bass_kernel_spmd(nc, [arrays], core_ids=[0])
    return r.results[0]["out"]
```
